# Optimizing a Trainium2 kernel written in Bass

```python
import numpy as np
import jax
import jax.numpy as jnp

def _softmax(x, axis=-1):
    return jax.nn.softmax(x, axis=axis)

def _gelu(x):
    return jax.nn.gelu(x, approximate=True)

def _silu(x):
    return jax.nn.silu(x)

def _sigmoid(x):
    return jax.nn.sigmoid(x)

def _layernorm(x, axis=-1, eps=1e-05):
    m = jnp.mean(x, axis=axis, keepdims=True)
    v = jnp.var(x, axis=axis, keepdims=True)
    return (x - m) / jnp.sqrt(v + eps)

def _scatter_add(tgt, idx, src, axis=0):
    return tgt.at[idx].add(src)

def _segment_sum(src, seg, n):
    return jax.ops.segment_sum(src, seg, n)
kernel_name = 'mk_xattn_ffn_d1_seqx_r8_16cc53'

def setup_inputs(seed: int=0):
    np.random.seed(seed)
    _w = jnp.asarray

    def _rec_inputs():
        import jax
        import jax.numpy as jnp
        _rk = jax.random.key(seed)
        x = 0.0003765 + 1 * jax.random.normal(jax.random.fold_in(_rk, 1), (64, 64, 128), jnp.float32)
        _lenS = 64 - jax.random.randint(jax.random.fold_in(_rk, 7), (64,), 0, max(1, 64 // 4) + 1, jnp.int32)
        _lenS2 = 64 - jax.random.randint(jax.random.fold_in(_rk, 8), (64,), 0, max(1, 64 // 4) + 1, jnp.int32)
        _ctx_1024P = jax.random.normal(jax.random.fold_in(_rk, 11), (64, 16, 128), jnp.float32)
        _ctx_1024c = jax.random.dirichlet(jax.random.fold_in(_rk, 511), 0.3 * jnp.ones((16,), jnp.float32), (64, 64))
        _ctx_1024t = jnp.einsum('bsk,bkd->bsd', _ctx_1024c, _ctx_1024P)
        _ctx_1024t = _ctx_1024t * jax.lax.rsqrt(jnp.mean(jnp.square(_ctx_1024t)) + 1e-12) * 0.953939
        ctx_1024 = -0.000292821 + 1.00034 * (_ctx_1024t + 0.3 * jax.random.normal(jax.random.fold_in(_rk, 611), (64, 64, 128), jnp.float32))
        _validS = jnp.arange(64)[None, :] < _lenS[:, None]
        _validS2 = jnp.arange(64)[None, :] < _lenS2[:, None]
        _causal = jnp.tril(jnp.ones((64, 64), dtype=bool))
        mask_BxS2_bf1 = jnp.ones((64, 64), dtype=bool)
        return (x, ctx_1024, mask_BxS2_bf1)
    x, ctx_1024, mask_BxS2_bf1 = _rec_inputs()

    def _L0_xattn_setup():
        import jax, jax.numpy as jnp
        import numpy as np
        B, S, SQ = (2, 256, 256)
        D_MODEL, H = (128, 16)
        DEPTH = D_MODEL // H
        key = jax.random.key(seed)
        ks = jax.random.split(key, 12)
        s = 1.0 / np.sqrt(D_MODEL)
        return {'value': jax.random.normal(ks[0], (B, S, D_MODEL), jnp.float32), 'key': jax.random.normal(ks[1], (B, S, D_MODEL), jnp.float32), 'query': jax.random.normal(ks[2], (B, SQ, D_MODEL), jnp.float32), 'key_padding_mask': jnp.ones((B, S), dtype=bool), 'Wq': jax.random.normal(ks[3], (D_MODEL, D_MODEL), jnp.float32) * s, 'bq': jnp.zeros((D_MODEL,), jnp.float32), 'Wk': jax.random.normal(ks[4], (D_MODEL, D_MODEL), jnp.float32) * s, 'bk': jnp.zeros((D_MODEL,), jnp.float32), 'Wv': jax.random.normal(ks[5], (D_MODEL, D_MODEL), jnp.float32) * s, 'bv': jnp.zeros((D_MODEL,), jnp.float32), 'Wo': jax.random.normal(ks[6], (D_MODEL, D_MODEL), jnp.float32) * s, 'bo': jnp.zeros((D_MODEL,), jnp.float32)}
    _L0_xattn_all = _L0_xattn_setup()
    _L0_xattn_in = {k: v for k, v in _L0_xattn_all.items() if k in ('Wq', 'bq', 'Wk', 'bk', 'Wv', 'bv', 'Wo', 'bo')}
    del _L0_xattn_all

    def _L0_ffn_setup():
        import jax, jax.numpy as jnp
        import numpy as np
        NUM_EXPERTS = 8
        CAP_FACTOR = 1.0
        MIN_CAP = 8
        key = jax.random.key(seed)
        ks = jax.random.split(key, 10)
        G, S, D, H, E = (4, 512, 128, 512, NUM_EXPERTS)
        s = 0.02
        return {'x': jax.random.normal(ks[0], (G, S, D), dtype=jnp.float32), 'gate': jax.random.normal(ks[1], (D, E), dtype=jnp.float32) * s, 'W1': jax.random.normal(ks[2], (E, D, H), dtype=jnp.float32) * s, 'b1': jnp.zeros((E, H), dtype=jnp.float32), 'W2': jax.random.normal(ks[3], (E, H, D), dtype=jnp.float32) * s, 'b2': jnp.zeros((E, D), dtype=jnp.float32), 'Ws1': jax.random.normal(ks[4], (D, H), dtype=jnp.float32) * s, 'bs1': jnp.zeros((H,), dtype=jnp.float32), 'Ws2': jax.random.normal(ks[5], (H, D), dtype=jnp.float32) * s, 'bs2': jnp.zeros((D,), dtype=jnp.float32)}
    _L0_ffn_all = _L0_ffn_setup()
    _L0_ffn_in = {k: v for k, v in _L0_ffn_all.items() if k in ('gate', 'W1', 'b1', 'W2', 'b2', 'Ws1', 'bs1', 'Ws2', 'bs2')}
    del _L0_ffn_all
    return {'x': x, 'ctx_1024': ctx_1024, 'mask_BxS2_bf1': mask_BxS2_bf1, 'L0_xattn_Wq': _L0_xattn_in['Wq'], 'L0_xattn_bq': _L0_xattn_in['bq'], 'L0_xattn_Wk': _L0_xattn_in['Wk'], 'L0_xattn_bk': _L0_xattn_in['bk'], 'L0_xattn_Wv': _L0_xattn_in['Wv'], 'L0_xattn_bv': _L0_xattn_in['bv'], 'L0_xattn_Wo': _L0_xattn_in['Wo'], 'L0_xattn_bo': _L0_xattn_in['bo'], 'L0_ffn_gate': _L0_ffn_in['gate'], 'L0_ffn_W1': _L0_ffn_in['W1'], 'L0_ffn_b1': _L0_ffn_in['b1'], 'L0_ffn_W2': _L0_ffn_in['W2'], 'L0_ffn_b2': _L0_ffn_in['b2'], 'L0_ffn_Ws1': _L0_ffn_in['Ws1'], 'L0_ffn_bs1': _L0_ffn_in['bs1'], 'L0_ffn_Ws2': _L0_ffn_in['Ws2'], 'L0_ffn_bs2': _L0_ffn_in['bs2']}

def reference(x, ctx_1024, mask_BxS2_bf1, L0_xattn_Wq, L0_xattn_bq, L0_xattn_Wk, L0_xattn_bk, L0_xattn_Wv, L0_xattn_bv, L0_xattn_Wo, L0_xattn_bo, L0_ffn_gate, L0_ffn_W1, L0_ffn_b1, L0_ffn_W2, L0_ffn_b2, L0_ffn_Ws1, L0_ffn_bs1, L0_ffn_Ws2, L0_ffn_bs2):
    import jax
    import jax.numpy as jnp

    def _L0_xattn_ref(value, key, query, key_padding_mask, Wq, bq, Wk, bk, Wv, bv, Wo, bo):
        import jax, jax.numpy as jnp
        import numpy as np
        B, S, SQ = (2, 256, 256)
        D_MODEL, H = (128, 16)
        DEPTH = D_MODEL // H
        b, sq = (query.shape[0], query.shape[1])
        q = (query @ Wq + bq).reshape(b, sq, H, DEPTH)
        k = (key @ Wk + bk).reshape(b, -1, H, DEPTH)
        v = (value @ Wv + bv).reshape(b, -1, H, DEPTH)
        logits = jnp.einsum('bqhd,bkhd->bhqk', q, k) / jnp.sqrt(jnp.asarray(DEPTH, q.dtype))
        logits = jnp.where(key_padding_mask[:, None, None, :], logits, jnp.asarray(-jnp.inf, logits.dtype))
        attn = jax.nn.softmax(logits, axis=-1)
        out = jnp.einsum('bhqk,bkhd->bqhd', attn, v).reshape(b, sq, D_MODEL)
        return out @ Wo + bo

    def _L0_ffn_ref(x, gate, W1, b1, W2, b2, Ws1, bs1, Ws2, bs2):
        import jax, jax.numpy as jnp
        import numpy as np
        NUM_EXPERTS = 8
        CAP_FACTOR = 1.0
        MIN_CAP = 8
        G, S, D = x.shape
        E = gate.shape[1]
        T = G * S
        capacity = max(MIN_CAP, int(CAP_FACTOR * T / E))
        logits = jnp.einsum('gsd,de->gse', x, gate)
        probs = jax.nn.softmax(logits, axis=-1)
        flat_probs = probs.transpose(2, 0, 1).reshape(E, T)
        scores, token_idx = jax.lax.top_k(flat_probs, k=capacity)
        scores = jnp.where(scores > -100000000.0, scores, 0.0)
        flat_x = x.reshape(T, D)
        tok = flat_x[token_idx]
        h = jax.nn.gelu(jnp.einsum('ecd,edh->ech', tok, W1) + b1[:, None, :])
        out_tok = jnp.einsum('ech,ehd->ecd', h, W2) + b2[:, None, :]
        scaled = out_tok * scores[..., None]
        routed = jnp.zeros_like(flat_x).at[token_idx.reshape(-1)].add(scaled.reshape(E * capacity, D)).reshape(G, S, D)
        shared = jax.nn.gelu(jnp.einsum('gsd,dh->gsh', x, Ws1) + bs1)
        shared = jnp.einsum('gsh,hd->gsd', shared, Ws2) + bs2
        return routed + shared
    x = x + _L0_xattn_ref(ctx_1024, ctx_1024, _layernorm(x, axis=-1), mask_BxS2_bf1, L0_xattn_Wq, L0_xattn_bq, L0_xattn_Wk, L0_xattn_bk, L0_xattn_Wv, L0_xattn_bv, L0_xattn_Wo, L0_xattn_bo)
    x = x + _L0_ffn_ref(_layernorm(x, axis=-1), L0_ffn_gate, L0_ffn_W1, L0_ffn_b1, L0_ffn_W2, L0_ffn_b2, L0_ffn_Ws1, L0_ffn_bs1, L0_ffn_Ws2, L0_ffn_bs2)
    return x

_drawn_inputs = setup_inputs


def setup_inputs(seed=0):
    import zlib

    import numpy as np

    out = dict(_drawn_inputs(seed))
    spreads = {'L0_xattn_bq': (0.0, 0.326),
     'L0_xattn_bk': (0.0, 0.8),
     'L0_xattn_bv': (0.0, 0.1),
     'L0_xattn_bo': (0.0, 0.1),
     'L0_ffn_b1': (0.0, 0.8),
     'L0_ffn_b2': (0.0, 0.546),
     'L0_ffn_bs1': (0.0, 0.427),
     'L0_ffn_bs2': (0.0, 0.1)}
    factors = {'L0_ffn_gate': 3.505, 'L0_ffn_W1': 7.043, 'L0_ffn_W2': 6.406}
    for name, (base, spread) in spreads.items():
        noise = np.random.default_rng([zlib.crc32(name.encode()), seed]).standard_normal(out[name].shape)
        drawn = base * np.exp(spread * noise) if base else spread * noise
        out[name] = jnp.asarray(drawn.astype(out[name].dtype))
    for name, factor in factors.items():
        out[name] = (out[name] * factor).astype(out[name].dtype)
    return out
```

```python
from contextlib import ExitStack

import numpy as np

import concourse.bass as bass
from concourse import mybir

F32 = mybir.dt.float32
BF16 = mybir.dt.bfloat16
I32 = mybir.dt.int32
U32 = mybir.dt.uint32
U8 = mybir.dt.uint8
ALU = mybir.AluOpType
ACT = mybir.ActivationFunctionType
AX = mybir.AxisListType

P = 128
B, S, D = 64, 64, 128
H, DH = 16, 8
T = B * S
NT = T // P
UT = 2
NU = NT // UT
E = 8
F = 512
NM = F // P
CAP = T // E
NI = CAP // P
FB = 512
NB = T // FB
EPS = 1e-5
MASKED = 1e30
SCALE = float(DH) ** -0.5
BITS = 30
SEARCH = BITS // 2
NA, NBL = 16, 32
ROW = D + E

C_ID, C_J, C_PM, C_ONZ, C_SAME, C_TRI = 0, 128, 132, 134, 166, 294
C_SEG, C_CV, C_IA, C_IB, C_P, C_ST, C_IND = 422, 678, 934, 950, 982, 983, 998
C_END = C_IND + 128
R_B1, R_BS1, R_B2, R_BS2, R_BQ, R_BK, R_BV, R_BO = 0, 32, 36, 44, 45, 46, 47, 48
NR = 49


def constants():
    r = np.arange(P)
    c = np.zeros((P, C_END), np.float32)
    c[:, C_ID:C_ID + P] = np.eye(P)
    c[:, C_J:C_J + 4] = (r[:, None] // DH) % 4 == np.arange(4)
    c[:, C_PM:C_PM + 2] = (r[:, None] // (2 * DH)) % 2 == np.arange(2)
    c[:, C_ONZ:C_ONZ + 32] = r[:, None] // 64 == (np.arange(32) // DH) % 2
    c[:, C_SAME:C_SAME + P] = r[:, None] % E == r % E
    c[:, C_TRI:C_TRI + P] = r[:, None] < r
    c[:, C_SEG:C_SEG + E * NT] = (np.arange(E * NT) % NT) != 0
    c[:, C_CV:C_CV + E * NT] = np.arange(E * NT) % NT
    c[:, C_IA:C_IA + NA] = np.arange(NA)
    c[:, C_IB:C_IB + NBL] = np.arange(NBL)
    c[:, C_P] = r
    c[:, C_ST:C_ST + SEARCH] = 2.0 ** (BITS - 2 - 2 * np.arange(SEARCH))
    c[0:2, C_IND:C_IND + P] = np.arange(2)[:, None] == r // 64
    k = (np.arange(1, 4)[None, :] << (BITS - 2 - 2 * np.arange(SEARCH))[:, None]).astype(np.int32)
    return c, np.broadcast_to(k.reshape(1, -1), (P, 3 * SEARCH)).copy()


def build(nc, x, ctx_in, mask, Wq, bq, Wk, bk, Wv, bv, Wo, bo, gate, W1, b1, W2, b2, Ws1, bs1, Ws2, bs2,
          consts, kbits, out, table, lists):
    es = ExitStack()
    with es:
        def sb(name, shape, dt=F32):
            return es.enter_context(nc.sbuf_tensor(name, shape, dt))

        def sem(name):
            return es.enter_context(nc.semaphore(name))

        cst = sb("cst", [P, C_END])
        kb = sb("kb", [P, SEARCH, 3], I32)
        ident = cst[:, C_ID:C_ID + P]
        bias_rows = sb("bias_rows", [NR, P])
        bias_c = sb("bias_c", [P, NR])
        bo2 = sb("bo2", [P, 1])
        wqkv = sb("wqkv", [P, 3, D])
        wo = sb("wo", [P, D])
        wom = sb("wom", [P, 2, D])
        gate_w = sb("gate_w", [P, E])
        mask8 = sb("mask8", [2, NT, S], U8)
        maskr = sb("maskr", [2, NT, S], BF16)
        ind = sb("ind", [2, P], BF16)
        same = sb("same", [P, P], BF16)
        tri = sb("tri", [P, P], BF16)
        ones = sb("ones", [P, P], BF16)
        iab = sb("iab", [P, NA + NBL], BF16)
        X = sb("X", [P, NT, D])
        cin = sb("cin", [P, 2, UT, D])
        st1 = sb("st1", [P, 2, UT, 6])
        mv1 = sb("mv1", [P, 2, UT, 2])
        rs1 = sb("rs1", [P, 2, UT])
        st2 = sb("st2", [P, 2, UT, 6])
        mv2 = sb("mv2", [P, 2, UT, 2])
        rs2 = sb("rs2", [P, 2, UT])
        mhalf = sb("mhalf", [P, UT])
        xh1 = sb("xh1", [P, 2, UT, D])
        xcT = sb("xcT", [P, 2, 2 * UT, P])
        QT = sb("QT", [P, 2, UT * P])
        KT = sb("KT", [P, 2, UT * P])
        Kbd = sb("Kbd", [P, 2, 4, UT * P])
        Vz = sb("Vz", [P, 2, 4, D])
        held = sb("held", [P, 2])
        mx = sb("mx", [P, 2, H])
        Pn = sb("Pn", [P, 2, 2, H * S])
        PTs = sb("PTs", [P, 2, 8, P])
        sums = sb("sums", [P, 2, H])
        rsum = sb("rsum", [P, 2, H])
        OLn = sb("OLn", [P, 2, 4, P])
        yTs = sb("yTs", [P, 2, UT * P])
        xh2 = sb("xh2", [P, 2, UT, D])
        x2Ts = sb("x2Ts", [P, 2, UT * P])
        X2T = sb("X2T", [P, T])
        lg = sb("lg", [P, NT, E])
        mxl = sb("mxl", [P, NT])
        pe_ = sb("pe_", [P, NT, E])
        sml = sb("sml", [P, NT])
        rsl = sb("rsl", [P, NT])
        pr8 = sb("pr8", [P, NT, E])
        prT = sb("prT", [P, 2 * P])
        cand = sb("cand", [P, 3], I32)
        cur = sb("cur", [P, 1], I32)
        junk = sb("junk", [P, 3, 2 * P], BF16)
        cnt = sb("cnt", [P, 3], BF16)
        junk3 = sb("junk3", [P, 3])
        nf = sb("nf", [P, 1])
        stepi = sb("stepi", [P, 1], I32)
        thr_b = sb("thr_b", [P, P])
        thr = sb("thr", [P, E])
        gtm = sb("gtm", [P, E, NT], BF16)
        eqm = sb("eqm", [P, E, NT], BF16)
        selm = sb("selm", [P, E, NT], BF16)
        scn = sb("scn", [P, E, NT])
        rk = sb("rk", [P, E, NT])
        rk2 = sb("rk2", [P, E, NT])
        gcn = sb("gcn", [P, E])
        need = sb("need", [P, E])
        posi = sb("posi", [P, E * NT], I32)
        pa = sb("pa", [P, E * NT], I32)
        pb = sb("pb", [P, E * NT], I32)
        pab = sb("pab", [P, E * NT], BF16)
        pbb = sb("pbb", [P, E * NT], BF16)
        Aoh = sb("Aoh", [P, E * NT, NA], BF16)
        Awt = sb("Awt", [P, E * NT, 2, NA], BF16)
        Boh = sb("Boh", [P, E * NT, NBL], BF16)
        tokp = sb("tokp", [NBL, E, NA])
        tokf = sb("tokf", [NBL, E, NA])
        toki = sb("toki", [NBL, NI, E, NI], I32)
        idx = sb("idx", [P, E, NI], U32)
        ws1 = sb("ws1", [P, F])
        ws2 = sb("ws2", [P, NM, D])
        w1 = sb("w1", [P, 2, F])
        w2 = sb("w2", [P, 2, NM, D])
        hT = sb("hT", [P, NM, FB])
        yT = sb("yT", [P, FB])
        yo = sb("yo", [P, 2, NI, D])
        gx = sb("gx", [P, 2, NI, ROW])
        xeT = sb("xeT", [P, 2, CAP])

        psS = es.enter_context(nc.psum_tensor("psS", [P, 4, 512], F32))
        psT = es.enter_context(nc.psum_tensor("psT", [P, 2, 512], F32))
        psO = es.enter_context(nc.psum_tensor("psO", [P, 512], F32))
        psJ = es.enter_context(nc.psum_tensor("psJ", [P, 512], F32))

        names = """c_ld br_ld w_ld m_ld wf_ld x_ld0 x_ld1 x_ld2 x_ld3 ctx_ld0 ctx_ld1 tab_st0 tab_st1
            pe_bias bias_ok bo2_mm bo2_ok cdve cpool mrow
            v_st1 v_ag1 v_ve1 pl_rs1 v_xh1 v_max v_sub v_sum v_rec a_o pl_pn v_x1 v_st2 v_ag2 v_ve2 pl_rs2 v_xh2
            v_gate v_v a_xt a_q a_k a_v a_exp a_pt a_y a_x2r a_x2t pl_kbd
            t_xt t_qk t_v t_S0 t_S t_T t_O t_y t_yt t_x2t t_g
            r_step r_p r_prT r_tT r_prs p_st s_cnt s_tot s_upd s_fin t_thr r_m r_ranks r_m2 r_ranks2 r_pos
            a_oh w_p w_c b_oh t_list r_tok l_st l_ld
            t_h a_h t_yy a_yy t_yo v_yo o_st0 o_st1 g_ld0 g_ld1 t_xe a_xe w_ld0 w_ld1 sc_st0 sc_st1""".split()
        q = {n: sem(n) for n in names}
        x_ld = [q[f"x_ld{k}"] for k in range(4)]
        ctx_ld = [q["ctx_ld0"], q["ctx_ld1"]]
        tab_st = [q["tab_st0"], q["tab_st1"]]
        g_ld = [q["g_ld0"], q["g_ld1"]]
        o_st = [q["o_st0"], q["o_st1"]]
        w_ldx = [q["w_ld0"], q["w_ld1"]]
        sc_st = [q["sc_st0"], q["sc_st1"]]

        x_v = x.rearrange("a s d -> (a s) d").rearrange("(c p) d -> p c d", p=P)
        ctx_v = ctx_in.rearrange("a s d -> (a s) d").rearrange("(c p) d -> p c d", p=P)
        out_rows = out.rearrange("a s d -> (a s) d")
        out_v = out_rows.rearrange("(c p) d -> p c d", p=P)
        tab_v = table.rearrange("(c p) w -> p c w", p=P)

        FIRST, LAST = -2, NU + 3
        LOOP0, NLOOP = 4, (NU - 3 - 4) // 2

        class Step:

            def __init__(self, i, u0, looped):
                self.i, self.u0, self.looped = i, u0, looped

            def u(self, k):
                return 2 * self.i + (self.u0 + k) if self.looped else self.u0 + k

            def half(self, k):
                return self.i + (self.u0 + k) // 2 if self.looped else (self.u0 + k) // 2

            def par(self, k):
                return (self.u0 + k) % 2

            def on(self, k):
                return self.looped or 0 <= self.u0 + k < NU

        def pipeline(eng, body):
            for u in range(FIRST, LOOP0):
                body(Step(0, u, False))
            with eng.Fori(0, NLOOP) as i:
                body(Step(i, LOOP0, True))
                body(Step(i, LOOP0 + 1, True))
            for u in range(LOOP0 + 2 * NLOOP, LAST):
                body(Step(0, u, False))

        def wait(eng, s, value):
            if not isinstance(value, int) or value > 0:
                eng.wait_ge(q[s] if isinstance(s, str) else s, value)

        block = es.enter_context(nc.Block())

        @block.sync
        def _(sp):
            sp.dma_start(cst[:], consts).then_inc(q["c_ld"], 16)
            for k in range(4):
                sp.dma_start(X[:, 8 * k:8 * k + 8, :], x_v[:, 8 * k:8 * k + 8, :]).then_inc(x_ld[k], 16)
                if k == 0:
                    for p in range(2):
                        sp.dma_start(cin[:, p], ctx_v[:, UT * p:UT * p + UT, :]).then_inc(ctx_ld[p], 16)

            def body(s):
                if s.on(3) and (s.looped or s.u0 + 3 >= 2):
                    wait(sp, "t_xt", s.u(2))
                    sp.dma_start(cin[:, s.par(3)], ctx_v[:, bass.ds(UT * s.u(3), UT), :]).then_inc(
                        ctx_ld[s.par(3)], 16)
                if s.on(-2):
                    wait(sp, "v_xh2", s.u(-1))
                    sp.dma_start(tab_v[:, bass.ds(UT * s.u(-2), UT), 0:D], xh2[:, s.par(-2)]).then_inc(
                        tab_st[s.par(-2)], 16)

            pipeline(sp, body)
            sp.wait_ge(q["r_p"], 1)
            sp.dma_start(tab_v[:, :, D:ROW], pr8[:]).then_inc(q["p_st"], 16)
            for b in range(NB):
                sp.wait_ge(q["v_yo"], b + 1)
                sp.dma_start(out_v[:, NI * b:NI * b + NI, :], yo[:, b % 2]).then_inc(o_st[b % 2], 16)
            for p in range(2):
                sp.wait_ge(o_st[p], 16 * (NB // 2))

        def y_evac(act, n):
            act.wait_ge(q["t_yy"], NM * (n + 1))
            wait(act, "t_yo", n)
            b = R_BS2 if n < NB else R_B2 + n - NB
            nc.scalar.activation(yT[:], psO[:], ACT.Identity, bias=bias_c[:, b:b + 1]).then_inc(q["a_yy"], 1)

        @block.scalar
        def _(act):
            act.dma_start(bias_rows[R_B1:R_B1 + E * NM, :], b1.rearrange("e (m p) -> (e m) p", p=P)).then_inc(q["br_ld"], 16)
            act.dma_start(bias_rows[R_BS1:R_BS1 + NM, :], bs1.rearrange("(m p) -> m p", p=P)).then_inc(q["br_ld"], 16)
            act.dma_start(bias_rows[R_B2:R_B2 + E, :], b2).then_inc(q["br_ld"], 16)
            for r, v in ((R_BS2, bs2), (R_BQ, bq), (R_BK, bk), (R_BV, bv), (R_BO, bo)):
                act.dma_start(bias_rows[r:r + 1, :], v.rearrange("(a d) -> a d", a=1)).then_inc(q["br_ld"], 16)
            for k, w in enumerate((Wq, Wk, Wv)):
                act.dma_start(wqkv[:, k, :], w).then_inc(q["w_ld"], 16)
            act.dma_start(wo[:], Wo).then_inc(q["w_ld"], 16)
            act.dma_start(gate_w[:], gate).then_inc(q["w_ld"], 16)
            act.dma_start(mask8[:], mask.rearrange("(i b) k -> b i k", b=2)).then_inc(q["m_ld"], 16)
            act.dma_start(kb[:], kbits.rearrange("p (s k) -> p s k", k=3)).then_inc(q["m_ld"], 16)
            act.dma_start(ws1[:], Ws1).then_inc(q["wf_ld"], 16)
            act.dma_start(ws2[:], Ws2.rearrange("(m p) d -> p m d", p=P)).then_inc(q["wf_ld"], 16)
            act.wait_ge(q["pe_bias"], 1)
            nc.scalar.copy(bias_c[:], psJ[:, 0:NR]).then_inc(q["bias_ok"], 1)
            act.wait_ge(q["bo2_mm"], 1)
            act.wait_ge(q["bias_ok"], 1)
            nc.scalar.activation(bo2[:], psJ[:, 0:1], ACT.Identity, bias=bias_c[:, R_BO:R_BO + 1]).then_inc(q["bo2_ok"], 1)

            def pt_evac(s, k, pr, hf):
                wait(act, "t_T", 4 * s.u(k) + 2 * pr + hf + 1)
                wait(act, "t_O", 2 * s.u(k) + pr - 1)
                nc.scalar.copy(PTs[:, pr, 4 * hf:4 * hf + 4, :], psT[:, hf].rearrange("p (a t) -> p a t", a=4)).then_inc(q["a_pt"], 1)

            def exps(s, pr):
                wait(act, "v_sub", 2 * s.u(0) + pr + 1)
                nc.scalar.activation(Pn[:, s.par(0), pr], Pn[:, s.par(0), pr], ACT.Exp, scale=SCALE).then_inc(q["a_exp"], 1)

            def body(s):
                if s.on(-2):
                    wait(act, "t_y", s.u(-1))
                    wait(act, "t_yt", s.u(-3))
                    nc.scalar.activation(yTs[:, s.par(-2)], psJ[:, 0:UT * P], ACT.Identity, bias=bo2[:, 0:1]).then_inc(q["a_y"], 1)
                if s.on(-1):
                    pt_evac(s, -1, 0, 0)
                    pt_evac(s, -1, 0, 1)
                if s.on(1):
                    wait(act, "t_xt", s.u(2))
                    wait(act, "t_v", s.u(0))
                    nc.scalar.copy(xcT[:, s.par(1)], psJ.rearrange("p (a t) -> p a t", a=4)).then_inc(q["a_xt"], 1)
                if s.on(-1):
                    pt_evac(s, -1, 1, 0)
                    pt_evac(s, -1, 1, 1)
                if s.on(-3):
                    wait(act, "t_x2t", s.u(-2))
                    wait(act, "t_g", s.u(-4))
                    nc.scalar.copy(X2T[:, bass.ds(UT * P * s.u(-3), UT * P)], psJ[:, 0:UT * P]).then_inc(q["a_x2r"], 1)
                    nc.scalar.copy(x2Ts[:, s.par(-3)], psJ[:, 0:UT * P]).then_inc(q["a_x2t"], 1)
                if s.on(0):
                    exps(s, 0)
                if s.on(1):
                    wait(act, "t_qk", s.u(2))
                    wait(act, "t_S", 2 * s.u(0))
                    nc.scalar.activation(QT[:, s.par(1)], psJ[:, 0:UT * P], ACT.Identity, bias=bias_c[:, R_BQ:R_BQ + 1]).then_inc(q["a_q"], 1)
                    wait(act, "pl_kbd", s.u(0))
                    nc.scalar.activation(KT[:, s.par(1)], psJ[:, UT * P:2 * UT * P], ACT.Identity, bias=bias_c[:, R_BK:R_BK + 1]).then_inc(q["a_k"], 1)
                if s.on(-1):
                    wait(act, "t_O", 2 * s.u(0))
                    wait(act, "t_y", s.u(-2))
                    nc.scalar.copy(OLn[:, s.par(-1)], psO.rearrange("p (b t) -> p b t", b=4)).then_inc(q["a_o"], 1)
                if s.on(0):
                    exps(s, 1)
                if s.on(1):
                    wait(act, "t_v", s.u(2))
                    wait(act, "t_O", 2 * s.u(0))
                    v = psJ[0:64, :].rearrange("p (b g h d) -> p b g h d", b=4, h=2, d=DH)
                    o = Vz[0:64, s.par(1)].rearrange("p b (g h d) -> p b g h d", h=2, d=DH)
                    nc.scalar.copy(o[:, :, :, 0, :], v[:, :, :, 0, :]).then_inc(q["a_v"], 1)

            act.wait_ge(q["cpool"], 2)
            pipeline(act, body)

            act.wait_ge(q["r_step"], 2)
            nc.scalar.activation(pe_[:], pe_[:], ACT.Exp).then_inc(q["r_prs"], 1)

            act.wait_ge(q["br_ld"], 16 * 8)
            for n in range(NB + E):
                e = n - NB
                if e == 0:
                    y_evac(act, n - 1)
                if e >= 0:
                    act.wait_ge(q["t_xe"], e + 1)
                    wait(act, "t_h", NM * (n - 1))
                    nc.scalar.copy(xeT[:, e % 2], psT[:, 1]).then_inc(q["a_xe"], 1)
                for m in range(NM):
                    if m == 2 and n > 0 and n != NB:
                        y_evac(act, n - 1)
                    act.wait_ge(q["t_h"], NM * n + m + 1)
                    wait(act, "t_yy", NM * (n - 1) + m + 1)
                    b = R_BS1 + m if e < 0 else R_B1 + NM * e + m
                    nc.scalar.activation(hT[:, m], psS[:, m], ACT.Gelu_apprx_tanh, bias=bias_c[:, b:b + 1]).then_inc(q["a_h"], 1)
            y_evac(act, NB + E - 1)

        @block.gpsimd
        def _(pool):
            nc.gpsimd.memset(mhalf[:], -0.5).then_inc(q["cpool"], 1)
            nc.gpsimd.memset(Vz[:], 0.0).then_inc(q["cpool"], 1)
            pool.wait_ge(q["c_ld"], 16)

            def normalise(s, pr):
                wait(pool, "v_rec", 2 * s.u(0) + pr + 1)
                pn = Pn[:, s.par(0), pr].rearrange("p (h k) -> p h k", k=S)
                nc.gpsimd.tensor_tensor(pn, pn, rsum[:, pr].unsqueeze(2).to_broadcast([P, H, S]), ALU.mult).then_inc(q["pl_pn"], 1)

            def body(s):
                if s.on(-2):
                    wait(pool, "v_ve2", s.u(-1))
                    wait(pool, "v_xh2", s.u(-3))
                    nc.gpsimd.tensor_tensor(rs2[:, s.par(-2)], mv2[:, s.par(-2), :, 1], mhalf[:], ALU.pow).then_inc(q["pl_rs2"], 1)
                if s.on(2):
                    wait(pool, "v_ve1", s.u(3))
                    wait(pool, "v_xh1", s.u(1))
                    nc.gpsimd.tensor_tensor(rs1[:, s.par(2)], mv1[:, s.par(2), :, 1], mhalf[:], ALU.pow).then_inc(q["pl_rs1"], 1)
                if s.on(0):
                    normalise(s, 0)
                if s.on(1):
                    wait(pool, "a_k", s.u(2))
                    wait(pool, "t_S", 2 * s.u(0))
                    nc.gpsimd.tensor_tensor(
                        Kbd[:, s.par(1)],
                        KT[:, s.par(1)].unsqueeze(1).to_broadcast([P, 4, UT * P]),
                        cst[:, C_J:C_J + 4].unsqueeze(2).to_broadcast([P, 4, UT * P]), ALU.mult).then_inc(q["pl_kbd"], 1)
                if s.on(0):
                    normalise(s, 1)

            pool.wait_ge(q["cpool"], 2)
            pipeline(pool, body)

            def load_w(e):
                pool.dma_start(w1[:, e % 2], W1[e]).then_inc(w_ldx[e % 2], 16)
                pool.dma_start(w2[:, e % 2], W2[e].rearrange("(m p) d -> p m d", p=P)).then_inc(w_ldx[e % 2], 16)

            load_w(0)
            load_w(1)
            pool.wait_ge(q["a_oh"], 1)
            nc.gpsimd.tensor_tensor(Awt[:, :, 1, :], Aoh[:], cst[:, C_CV:C_CV + E * NT].unsqueeze(2).to_broadcast([P, E * NT, NA]),
                                    ALU.mult).then_inc(q["w_c"], 1)
            pool.wait_ge(q["r_tok"], 3)
            pool.dma_start(lists.rearrange("(b k) -> b k", b=NBL), toki[:].rearrange("b a e i -> b (a e i)")).then_inc(q["l_st"], 16)
            pool.wait_ge(q["l_st"], 16)
            pool.dma_start(idx[:], lists.bitcast(U32).rearrange("(p e i) -> p e i", p=P, e=E)).then_inc(q["l_ld"], 16)
            pool.wait_ge(q["l_ld"], 16)
            for p in range(2):
                pool.wait_ge(tab_st[p], 16 * (NU // 2))
            pool.wait_ge(q["p_st"], 16)

            def gather(e):
                if e >= 2:
                    pool.wait_ge(q["v_yo"], NB + e - 1)
                for i in range(NI):
                    pool.indirect_dma_start(
                        out=gx[:, e % 2, i, :], out_offset=None, in_=table[:, :],
                        in_offset=bass.IndirectOffsetOnAxis(ap=idx[:, e, i:i + 1], axis=0)).then_inc(g_ld[e % 2], 16)

            gather(0)
            gather(1)
            for p in range(2):
                pool.wait_ge(o_st[p], 16 * (NB // 2))
            for e in range(E):
                pool.wait_ge(q["v_yo"], NB + e + 1)
                if e:
                    pool.wait_ge(sc_st[(e - 1) % 2], 16 * NI * ((e - 1) // 2 + 1))
                for i in range(NI):
                    pool.indirect_dma_start(
                        out=out_rows, out_offset=bass.IndirectOffsetOnAxis(ap=idx[:, e, i:i + 1], axis=0),
                        in_=yo[:, e % 2, i, :], in_offset=None, compute_op=ALU.add).then_inc(sc_st[e % 2], 16)
                if e + 2 < E:
                    gather(e + 2)
                    pool.wait_ge(q["t_yy"], NM * (NB + e + 1))
                    load_w(e + 2)
            for p in range(2):
                pool.wait_ge(sc_st[p], 16 * NI * (E // 2))

        @block.vector
        def _(dve):
            dve.wait_ge(q["c_ld"], 16)
            nc.vector.tensor_copy(ind[:], cst[0:2, C_IND:C_IND + P]).then_inc(q["cdve"], 1)
            nc.vector.tensor_copy(same[:], cst[:, C_SAME:C_SAME + P]).then_inc(q["cdve"], 1)
            nc.vector.tensor_copy(tri[:], cst[:, C_TRI:C_TRI + P]).then_inc(q["cdve"], 1)
            nc.vector.memset(ones[:], 1.0).then_inc(q["cdve"], 1)
            nc.vector.tensor_copy(iab[:], cst[:, C_IA:C_IA + NA + NBL]).then_inc(q["cdve"], 1)
            dve.wait_ge(q["w_ld"], 16 * 5)
            for k in range(2):
                nc.vector.tensor_scalar(wom[:, k], wo[:], cst[:, C_PM + k:C_PM + k + 1], None, ALU.mult).then_inc(q["cdve"], 1)
            dve.wait_ge(q["m_ld"], 32)
            nc.vector.tensor_scalar(maskr[:], mask8[:], 1.0, MASKED, ALU.subtract, ALU.mult).then_inc(q["mrow"], 1)
            for k in range(4):
                dve.wait_ge(x_ld[k], 16)

            def stats(v, par, c0, st, mv, n_st, n_ag, n_ve):
                nc.vector.memset(held[:, 0:1], 0.0)
                for t in range(UT):
                    nc.vector.bn_stats(st[:, par, t], X[:, bass.ds(c0 + t, 1), :].rearrange("p a d -> p (a d)")).then_inc(q[n_st], 1)
                wait(dve, n_st, UT * (v + 1))
                nc.vector.memset(held[:, 1:2], 0.0)
                for t in range(UT):
                    nc.vector.bn_aggr(mv[:, par, t], st[:, par, t]).then_inc(q[n_ag], 1)
                wait(dve, n_ag, UT * (v + 1))
                nc.vector.tensor_scalar(mv[:, par, :, 1], mv[:, par, :, 1], EPS, None, ALU.add).then_inc(q[n_ve], 1)

            def normed(dst, par, c0, mv, rs, name):
                for t in range(UT):
                    ins = nc.vector.tensor_scalar(dst[:, par, t], X[:, bass.ds(c0 + t, 1), :].rearrange("p a d -> p (a d)"),
                                                  mv[:, par, t, 0:1], rs[:, par, t:t + 1], ALU.subtract, ALU.mult)
                ins.then_inc(q[name], 1)

            def centre(s, pr):
                wait(dve, "t_S", 2 * s.u(0) + pr + 1)
                z = psS[:, 2 * pr:2 * pr + 2, :].rearrange("p a (h k) -> p (a h) k", k=S)
                nc.vector.tensor_reduce(mx[:, pr], z, AX.X, ALU.max).then_inc(q["v_max"], 1)
                wait(dve, "v_max", 2 * s.u(0) + pr + 1)
                wait(dve, "t_T", 4 * s.u(-2) + 2 * pr + 2)
                nc.vector.tensor_tensor(Pn[:, s.par(0), pr].rearrange("p (h k) -> p h k", k=S), z,
                                        mx[:, pr].unsqueeze(2).to_broadcast([P, H, S]), ALU.subtract).then_inc(q["v_sub"], 1)

            def row_sums(s, pr):
                n = 2 * s.u(0) + pr + 1
                wait(dve, "a_exp", n)
                nc.vector.tensor_reduce(sums[:, pr], Pn[:, s.par(0), pr].rearrange("p (h k) -> p h k", k=S), AX.X, ALU.add).then_inc(q["v_sum"], 1)
                wait(dve, "v_sum", n)
                wait(dve, "pl_pn", n - 2)
                nc.vector.reciprocal(rsum[:, pr], sums[:, pr]).then_inc(q["v_rec"], 1)

            def body(s):
                if s.on(-2):
                    wait(dve, "t_yt", s.u(-1))
                    xs = X[:, bass.ds(UT * s.u(-2), UT), :].rearrange("p a d -> p (a d)")
                    nc.vector.tensor_tensor(xs, xs, psJ[:, 0:UT * P], ALU.add).then_inc(q["v_x1"], 1)
                if s.on(0):
                    centre(s, 0)
                if s.on(-2):
                    wait(dve, "v_x1", s.u(-1))
                    stats(s.u(-2), s.par(-2), UT * s.u(-2), st2, mv2, "v_st2", "v_ag2", "v_ve2")
                if s.on(0):
                    centre(s, 1)
                if s.on(2):
                    stats(s.u(2), s.par(2), UT * s.u(2), st1, mv1, "v_st1", "v_ag1", "v_ve1")
                if s.on(0):
                    row_sums(s, 0)
                if s.on(-2):
                    wait(dve, "pl_rs2", s.u(-1))
                    wait(dve, "t_x2t", s.u(-3))
                    wait(dve, tab_st[s.par(-2)], 16 * s.half(-2))
                    normed(xh2, s.par(-2), UT * s.u(-2), mv2, rs2, "v_xh2")
                if s.on(-3):
                    wait(dve, "t_g", s.u(-2))
                    nc.vector.tensor_copy(lg[:, bass.ds(UT * s.u(-3), UT), :].rearrange("p a e -> p (a e)"), psT[:, 0, 0:UT * E]).then_inc(q["v_gate"], 1)
                if s.on(1):
                    wait(dve, "t_v", s.u(2))
                    wait(dve, "t_O", 2 * s.u(0))
                    v = psJ[64:128, :].rearrange("p (b g h d) -> p b g h d", b=4, h=2, d=DH)
                    o = Vz[64:128, s.par(1)].rearrange("p b (g h d) -> p b g h d", h=2, d=DH)
                    nc.vector.tensor_copy(o[:, :, :, 1, :], v[:, :, :, 1, :]).then_inc(q["v_v"], 1)
                if s.on(0):
                    row_sums(s, 1)
                if s.on(2):
                    wait(dve, "pl_rs1", s.u(3))
                    wait(dve, "t_xt", s.u(1))
                    normed(xh1, s.par(2), UT * s.u(2), mv1, rs1, "v_xh1")

            dve.wait_ge(q["cpool"], 2)
            pipeline(dve, body)

            dve.wait_ge(q["v_gate"], NU)
            nc.vector.tensor_reduce(mxl[:], lg[:], AX.X, ALU.max).then_inc(q["r_step"], 1)
            dve.wait_ge(q["r_step"], 1)
            nc.vector.tensor_tensor(pe_[:], lg[:], mxl[:].unsqueeze(2).to_broadcast([P, NT, E]), ALU.subtract).then_inc(q["r_step"], 1)
            dve.wait_ge(q["r_prs"], 1)
            nc.vector.tensor_reduce(sml[:], pe_[:], AX.X, ALU.add).then_inc(q["r_step"], 1)
            dve.wait_ge(q["r_step"], 3)
            nc.vector.reciprocal(rsl[:], sml[:]).then_inc(q["r_step"], 1)
            dve.wait_ge(q["r_step"], 4)
            nc.vector.tensor_tensor(pr8[:], pe_[:], rsl[:].unsqueeze(2).to_broadcast([P, NT, E]), ALU.mult).then_inc(q["r_p"], 1)
            dve.wait_ge(q["r_tT"], 1)
            nc.vector.tensor_copy(prT[:], psT[:, 1, 0:2 * P]).then_inc(q["r_prT"], 1)
            nc.vector.memset(cur[:], 0).then_inc(q["s_upd"], 1)
            nc.vector.tensor_copy(cand[:], kb[:, 0]).then_inc(q["s_upd"], 1)
            dve.wait_ge(q["r_prT"], 1)

            def shared_out(b):
                dve.wait_ge(q["t_yo"], b + 1)
                if b >= 2:
                    dve.wait_ge(o_st[b % 2], 16 * (b // 2))
                nc.vector.tensor_tensor(yo[:, b % 2], psT[:, 0].rearrange("p (a d) -> p a d", a=NI),
                                        X[:, NI * b:NI * b + NI, :], ALU.add).then_inc(q["v_yo"], 1)

            for k in range(SEARCH):
                dve.wait_ge(q["s_upd"], 2 + 4 * k)
                if k:
                    dve.wait_ge(q["s_tot"], k)
                for j in range(3):
                    with nc.allow_low_precision(reason="counts up to 256 are exact"):
                        ins = nc.vector.tensor_scalar(junk[:, j], prT[:], cand[:, j:j + 1].bitcast(F32), 0.0, ALU.is_ge, ALU.add,
                                                      accum_out=cnt[:, j:j + 1])
                    ins.then_inc(q["s_cnt"], 1)
                dve.wait_ge(q["s_tot"], k + 1)
                nc.vector.tensor_scalar(junk3[:], psT[:, 1, 0:3], float(CAP), 0.0, ALU.is_ge, ALU.add,
                                        accum_out=nf[:]).then_inc(q["s_upd"], 1)
                dve.wait_ge(q["s_upd"], 2 + 4 * k + 1)
                nc.vector.tensor_scalar(stepi[:], nf[:], cst[:, C_ST + k:C_ST + k + 1], None, ALU.mult).then_inc(q["s_upd"], 1)
                dve.wait_ge(q["s_upd"], 2 + 4 * k + 2)
                nc.vector.tensor_tensor(cur[:], cur[:], stepi[:], ALU.bitwise_or).then_inc(q["s_upd"], 1)
                dve.wait_ge(q["s_upd"], 2 + 4 * k + 3)
                if k + 1 < SEARCH:
                    nc.vector.tensor_tensor(cand[:], kb[:, k + 1], cur[:].to_broadcast([P, 3]), ALU.bitwise_or).then_inc(q["s_upd"], 1)
                if k % 2 and k >= 3:
                    shared_out((k - 3) // 2)
            shared_out(NB - 2)
            nc.vector.tensor_copy(thr_b[:], cur[:].bitcast(F32).to_broadcast([P, P])).then_inc(q["s_fin"], 1)
            dve.wait_ge(q["t_thr"], 1)
            nc.vector.tensor_copy(thr[:], psT[:, 1, 0:E]).then_inc(q["s_fin"], 1)
            dve.wait_ge(q["s_fin"], 2)
            tb = thr[:].unsqueeze(1).to_broadcast([P, NT, E])
            nc.vector.tensor_tensor(gtm[:].rearrange("p e c -> p c e"), pr8[:], tb, ALU.is_gt).then_inc(q["r_m"], 1)
            nc.vector.tensor_tensor(eqm[:].rearrange("p e c -> p c e"), pr8[:], tb, ALU.is_equal).then_inc(q["r_m"], 1)

            def ranks(name, tri_tot):
                before, tot = psJ[:, 0:E * NT], psJ[:, E * NT:2 * E * NT]
                nc.vector.tensor_tensor_scan(scn[:].rearrange("p e c -> p (e c)"), cst[:, C_SEG:C_SEG + E * NT], tot, 0.0,
                                             ALU.mult, ALU.add).then_inc(q[name], 1)
                dve.wait_ge(q[name], 1)
                nc.vector.tensor_tensor(rk[:].rearrange("p e c -> p (e c)"), scn[:].rearrange("p e c -> p (e c)"), before, ALU.add).then_inc(q[name], 1)
                dve.wait_ge(q[name], 2)
                nc.vector.tensor_tensor(rk2[:].rearrange("p e c -> p (e c)"), rk[:].rearrange("p e c -> p (e c)"), tot, ALU.subtract).then_inc(q[name], 1)
                dve.wait_ge(q[name], 3)

            dve.wait_ge(q["r_ranks"], 1)
            ranks("r_m2", None)
            nc.vector.tensor_reduce(gcn[:], psT[:, 1, 0:E * NT].rearrange("p (e c) -> p e c", e=E), AX.X, ALU.add).then_inc(q["r_m2"], 1)
            dve.wait_ge(q["r_m2"], 4)
            nc.vector.tensor_scalar(need[:], gcn[:], -1.0, float(CAP), ALU.mult, ALU.add).then_inc(q["r_m2"], 1)
            dve.wait_ge(q["r_m2"], 5)
            nc.vector.tensor_tensor(rk[:], rk2[:], need[:].unsqueeze(2).to_broadcast([P, E, NT]), ALU.is_lt).then_inc(q["r_m2"], 1)
            dve.wait_ge(q["r_m2"], 6)
            nc.vector.tensor_tensor(rk2[:], rk[:], eqm[:], ALU.mult).then_inc(q["r_m2"], 1)
            dve.wait_ge(q["r_m2"], 7)
            nc.vector.tensor_tensor(selm[:], rk2[:], gtm[:], ALU.add).then_inc(q["r_m"], 1)
            dve.wait_ge(q["r_ranks"], 2)
            dve.wait_ge(q["r_m"], 3)
            ranks("r_ranks2", None)
            nc.vector.tensor_scalar(rk[:], selm[:], -2.0 * CAP, 2.0 * CAP, ALU.mult, ALU.add).then_inc(q["r_ranks2"], 1)
            dve.wait_ge(q["r_ranks2"], 4)
            nc.vector.tensor_tensor(posi[:], rk[:].rearrange("p e c -> p (e c)"), rk2[:].rearrange("p e c -> p (e c)"), ALU.add).then_inc(q["r_ranks2"], 1)
            dve.wait_ge(q["r_ranks2"], 5)
            nc.vector.tensor_scalar(pa[:], posi[:], 5, None, ALU.logical_shift_right).then_inc(q["r_ranks2"], 1)
            nc.vector.tensor_scalar(pb[:], posi[:], NBL - 1, None, ALU.bitwise_and).then_inc(q["r_ranks2"], 1)
            dve.wait_ge(q["r_ranks2"], 6)
            nc.vector.tensor_copy(pab[:], pa[:]).then_inc(q["r_pos"], 1)
            dve.wait_ge(q["r_ranks2"], 7)
            nc.vector.tensor_copy(pbb[:], pb[:]).then_inc(q["r_pos"], 1)
            dve.wait_ge(q["r_pos"], 2)
            nc.vector.tensor_tensor(Aoh[:], iab[:, 0:NA].unsqueeze(1).to_broadcast([P, E * NT, NA]),
                                    pab[:].unsqueeze(2).to_broadcast([P, E * NT, NA]), ALU.is_equal).then_inc(q["a_oh"], 1)
            nc.vector.tensor_tensor(Boh[:], iab[:, NA:NA + NBL].unsqueeze(1).to_broadcast([P, E * NT, NBL]),
                                    pbb[:].unsqueeze(2).to_broadcast([P, E * NT, NBL]), ALU.is_equal).then_inc(q["b_oh"], 1)
            dve.wait_ge(q["a_oh"], 1)
            nc.vector.tensor_scalar(Awt[:, :, 0, :], Aoh[:], cst[:, C_P:C_P + 1], None, ALU.mult).then_inc(q["w_p"], 1)
            shared_out(NB - 1)
            dve.wait_ge(q["t_list"], 1)
            li = psJ[0:NBL, 0:E * 2 * NA].rearrange("b (e k a) -> b e k a", e=E, k=2)
            nc.vector.tensor_copy(tokp[:], li[:, :, 0, :]).then_inc(q["r_tok"], 1)
            dve.wait_ge(q["r_tok"], 1)
            nc.vector.scalar_tensor_tensor(out=tokf[:], in0=li[:, :, 1, :], scalar=float(P), in1=tokp[:], op0=ALU.mult, op1=ALU.add).then_inc(q["r_tok"], 1)
            dve.wait_ge(q["r_tok"], 2)
            nc.vector.tensor_copy(toki[:].rearrange("b a e i -> b e a i"), tokf[:].rearrange("b e (a i) -> b e a i", i=NI)).then_inc(q["r_tok"], 1)
            for e in range(E):
                dve.wait_ge(q["t_yo"], NB + e + 1)
                dve.wait_ge(g_ld[e % 2], 16 * NI * (e // 2 + 1))
                if e < 2:
                    dve.wait_ge(o_st[e % 2], 16 * (NB // 2))
                else:
                    dve.wait_ge(sc_st[e % 2], 16 * NI * (e // 2))
                nc.vector.tensor_tensor(yo[:, e % 2], psT[:, 0].rearrange("p (a d) -> p a d", a=NI),
                                        gx[:, e % 2, :, D + e:D + e + 1].to_broadcast([P, NI, D]), ALU.mult).then_inc(q["v_yo"], 1)

        @block.tensor
        def _(pe):
            mm, tr = nc.tensor.matmul, nc.tensor.transpose
            pe.wait_ge(q["c_ld"], 16)
            pe.wait_ge(q["br_ld"], 16 * 8)
            tr(psJ[:, 0:NR], bias_rows[:], ident[0:NR, 0:NR]).then_inc(q["pe_bias"], 1)
            pe.wait_ge(q["bias_ok"], 1)
            pe.wait_ge(q["w_ld"], 16 * 5)
            mm(psJ[:, 0:1], wo[:], bias_c[:, R_BV:R_BV + 1], start=True, stop=True).then_inc(q["bo2_mm"], 1)
            pe.wait_ge(q["bo2_ok"], 1)
            pe.wait_ge(q["cdve"], 7)
            pe.wait_ge(q["mrow"], 1)

            def mask_rows(s):
                for bank in range(4):
                    m = maskr[:, bass.ds(UT * s.u(0) + bank // 2, 1), :].to_broadcast([2, 8, S])
                    mm(psS[:, bank], ind[:], m, start=True, stop=False, skip_group_check=True)

            def logits(s, step):
                p = s.par(0)
                for pr, g in ((0, step), (0, 2 + step), (1, 1 - step), (1, 3 - step)):
                    for b in range(2):
                        r, c = 32 * g, P * pr + 64 * b
                        ins = mm(psS[64 * b:64 * b + 64, 2 * pr + g // 2, 256 * (g % 2):256 * (g % 2) + 256],
                                 QT[r:r + 32, p, c:c + 64], Kbd[r:r + 32, p, :, c:c + 64], start=False, stop=(step == 1),
                                 tile_position=(r, 64 * b), skip_group_check=True)
                    if step == 1 and g in (3, 2):
                        ins.then_inc(q["t_S"], 1)
                if step == 0:
                    ins.then_inc(q["t_S0"], 1)

            def p_transpose(s, pr, hf):
                v = 4 * s.u(-1) + 2 * pr + hf
                wait(pe, "pl_pn", 2 * s.u(-1) + pr + 1)
                wait(pe, "a_pt", v - 1)
                for a in range(4):
                    k = 4 * hf + a
                    ins = tr(psT[:, hf, P * a:P * a + P], Pn[:, s.par(-1), pr, P * k:P * k + P], ident)
                ins.then_inc(q["t_T"], 1)

            def p_v(s, pr):
                wait(pe, "a_pt", 4 * s.u(-1) + 2 * pr + 2)
                wait(pe, "a_v", s.u(0))
                wait(pe, "v_v", s.u(0))
                wait(pe, "a_o", s.u(-1))
                for b in range(2):
                    for t in range(4):
                        o = P * (2 * pr + b)
                        ins = mm(psO[32 * t:32 * t + 32, o:o + P], Vz[:, s.par(-1), 2 * pr + b, 32 * t:32 * t + 32],
                                 PTs[:, pr, 2 * t:2 * t + 2, 64 * b:64 * b + 64], start=True, stop=True,
                                 tile_position=(0, 32 * t), skip_group_check=True)
                ins.then_inc(q["t_O"], 1)

            def body(s):
                if s.on(0):
                    wait(pe, "v_sub", 2 * s.u(0))
                    wait(pe, "a_q", s.u(1))
                    wait(pe, "pl_kbd", s.u(1))
                    mask_rows(s)
                    logits(s, 0)
                if s.on(0):
                    wait(pe, "a_v", s.u(1))
                    wait(pe, "v_v", s.u(1))
                if s.on(-2):
                    if not s.on(0):
                        wait(pe, "a_x2t", s.u(-3))
                    wait(pe, "a_o", s.u(-1))
                    for k in range(2):
                        ins = mm(psJ[:, 0:UT * P], wom[:, k], OLn[:, s.par(-2), :, 64 * k:64 * k + 64], start=(k == 0), stop=(k == 1))
                    ins.then_inc(q["t_y"], 1)
                if s.on(0):
                    wait(pe, "t_S0", s.u(1))
                    logits(s, 1)
                if s.on(-2):
                    wait(pe, "a_y", s.u(-1))
                    for t in range(UT):
                        ins = tr(psJ[:, P * t:P * t + P], yTs[:, s.par(-2), P * t:P * t + P], ident)
                    ins.then_inc(q["t_yt"], 1)
                if s.on(-1):
                    wait(pe, "v_gate", s.u(-3))
                    p_transpose(s, 0, 0)
                    p_transpose(s, 0, 1)
                if s.on(1):
                    wait(pe, "v_x1", s.u(-1))
                    wait(pe, "v_xh1", s.u(2))
                    wait(pe, ctx_ld[s.par(1)], 16 * (s.half(1) + 1))
                    for t in range(UT):
                        tr(psJ[:, P * t:P * t + P], xh1[:, s.par(1), t], ident)
                    for t in range(UT):
                        ins = tr(psJ[:, P * (UT + t):P * (UT + t) + P], cin[:, s.par(1), t], ident)
                    ins.then_inc(q["t_xt"], 1)
                if s.on(-1):
                    p_transpose(s, 1, 0)
                    p_transpose(s, 1, 1)
                if s.on(-3):
                    if s.on(1):
                        wait(pe, "a_xt", s.u(2))
                    elif s.on(-2):
                        wait(pe, "v_x1", s.u(-1))
                    wait(pe, "v_xh2", s.u(-2))
                    for t in range(UT):
                        ins = tr(psJ[:, P * t:P * t + P], xh2[:, s.par(-3), t], ident)
                    ins.then_inc(q["t_x2t"], 1)
                if s.on(-1):
                    p_v(s, 0)
                if s.on(1):
                    wait(pe, "a_x2t", s.u(-2))
                    wait(pe, "a_xt", s.u(2))
                    for k in range(2):
                        ins = mm(psJ[:, UT * P * k:UT * P * (k + 1)], wqkv[:, k], xcT[:, s.par(1), UT * k:UT * k + UT], start=True, stop=True)
                    ins.then_inc(q["t_qk"], 1)
                if s.on(-1):
                    p_v(s, 1)
                if s.on(-3):
                    wait(pe, "a_x2t", s.u(-2))
                    wait(pe, "a_pt", 4 * s.u(0) - 1 if s.on(-1) else 4 * NU)
                    if not s.on(-1):
                        wait(pe, "v_gate", s.u(-3))
                    for t in range(UT):
                        ins = mm(psT[:, 0, E * t:E * t + E], x2Ts[:, s.par(-3), P * t:P * t + P], gate_w[:], start=True, stop=True)
                    ins.then_inc(q["t_g"], 1)
                if s.on(1):
                    wait(pe, "a_k", s.u(2))
                    wait(pe, "a_q", s.u(2))
                    for b in range(4):
                        cT = xcT[:, s.par(1), UT + b // 2, 64 * (b % 2):64 * (b % 2) + 64]
                        for h in range(2):
                            ins = mm(psJ[64 * h:64 * h + 64, P * b:P * b + P], cT, wqkv[:, 2], start=True, stop=True,
                                     tile_position=(0, 64 * h), skip_group_check=True)
                    ins.then_inc(q["t_v"], 1)

            pipeline(pe, body)

            def hidden(n, m):
                e = n - NB
                if n == 0:
                    pe.wait_ge(q["v_sub"], 2 * NU)
                    if m == 0:
                        pe.wait_ge(q["a_x2r"], NU)
                        pe.wait_ge(q["wf_ld"], 32)
                else:
                    pe.wait_ge(q["a_h"], NM * (n - 1) + m + 1)
                if e >= 0 and m == 0:
                    pe.wait_ge(q["a_xe"], e + 1)
                    pe.wait_ge(w_ldx[e % 2], 32 * (e // 2 + 1))
                w = ws1[:, P * m:P * m + P] if e < 0 else w1[:, e % 2, P * m:P * m + P]
                src = X2T[:, FB * n:FB * n + FB] if e < 0 else xeT[:, e % 2]
                mm(psS[:, m], w, src, start=True, stop=True).then_inc(q["t_h"], 1)

            def second(n, m):
                pe.wait_ge(q["a_h"], NM * n + m + 1)
                if m == 0:
                    wait(pe, "a_yy", n)
                    if n == 0:
                        pe.wait_ge(q["a_o"], NU)
                w = ws2[:, m] if n < NB else w2[:, (n - NB) % 2, m]
                mm(psO[:], w, hT[:, m], start=(m == 0), stop=(m == NM - 1)).then_inc(q["t_yy"], 1)

            def turn_back(n):
                pe.wait_ge(q["a_yy"], n + 1)
                if n == 0:
                    pe.wait_ge(q["v_gate"], NU)
                wait(pe, "v_yo", n)
                for i in range(NI):
                    ins = tr(psT[:, 0, P * i:P * i + P], yT[:, P * i:P * i + P], ident)
                ins.then_inc(q["t_yo"], 1)

            def search(k):
                if k == 0:
                    pe.wait_ge(q["r_p"], 1)
                    for h in range(2):
                        ins = tr(psT[:, 1, P * h:P * h + P], pr8[:, 16 * h:16 * h + 16, :].rearrange("p c e -> p (c e)"), ident)
                    ins.then_inc(q["r_tT"], 1)
                    pe.wait_ge(q["r_prT"], 1)
                if k < SEARCH:
                    pe.wait_ge(q["s_cnt"], 3 * (k + 1))
                    if k:
                        pe.wait_ge(q["s_upd"], 2 + 4 * (k - 1) + 1)
                    mm(psT[:, 1, 0:3], same[:], cnt[:], start=True, stop=True).then_inc(q["s_tot"], 1)

            def gather_in(e):
                pe.wait_ge(g_ld[e % 2], 16 * NI * (e // 2 + 1))
                wait(pe, "a_xe", e)
                for i in range(NI):
                    ins = tr(psT[:, 1, P * i:P * i + P], gx[:, e % 2, i, 0:D], ident)
                ins.then_inc(q["t_xe"], 1)

            def block_of(n, slots):
                hidden(n, 0)
                if n and n != NB:
                    second(n - 1, 2)
                slots[0]()
                hidden(n, 1)
                if n and n != NB:
                    second(n - 1, 3)
                slots[1]()
                hidden(n, 2)
                if n and n != NB:
                    turn_back(n - 1)
                second(n, 0)
                slots[2]()
                hidden(n, 3)
                second(n, 1)
                slots[3]()

            none = lambda: None
            for n in range(NB):
                k = 2 * n
                block_of(n, [none, (lambda k=k: search(k)), none, (lambda k=k: search(k + 1))])
            second(NB - 1, 2)
            second(NB - 1, 3)
            turn_back(NB - 1)

            pe.wait_ge(q["s_fin"], 1)
            tr(psT[:, 1, 0:P], thr_b[:], ident).then_inc(q["t_thr"], 1)
            pe.wait_ge(q["r_m"], 2)
            fl = lambda a: a[:].rearrange("p e c -> p (e c)")
            pe.wait_ge(q["a_x2t"], NU)
            mm(psJ[:, 0:E * NT], tri[:], fl(eqm), start=True, stop=True)
            mm(psJ[:, E * NT:2 * E * NT], ones[:], fl(eqm), start=True, stop=True)
            mm(psT[:, 1, 0:E * NT], ones[:], fl(gtm), start=True, stop=True).then_inc(q["r_ranks"], 1)
            pe.wait_ge(q["r_m"], 3)
            mm(psJ[:, 0:E * NT], tri[:], fl(selm), start=True, stop=True)
            mm(psJ[:, E * NT:2 * E * NT], ones[:], fl(selm), start=True, stop=True).then_inc(q["r_ranks"], 1)
            pe.wait_ge(q["w_p"], 1)
            pe.wait_ge(q["w_c"], 1)
            pe.wait_ge(q["b_oh"], 1)
            pe.wait_ge(q["r_ranks2"], 3)
            for e in range(E):
                for c in range(NT):
                    ins = mm(psJ[0:NBL, 2 * NA * e:2 * NA * (e + 1)], Boh[:, NT * e + c, :], Awt[:, NT * e + c].rearrange("p k a -> p (k a)"),
                             start=(c == 0), stop=(c == NT - 1), skip_group_check=True)
            ins.then_inc(q["t_list"], 1)

            gather_in(0)
            for e in range(E):
                nxt = (lambda e=e: gather_in(e + 1)) if e + 1 < E else none
                block_of(NB + e, [none, none, nxt, none])
            second(NB + E - 1, 2)
            second(NB + E - 1, 3)
            turn_back(NB + E - 1)


_INS = ['x', 'ctx_1024', 'mask_BxS2_bf1', 'L0_xattn_Wq', 'L0_xattn_bq', 'L0_xattn_Wk', 'L0_xattn_bk', 'L0_xattn_Wv',
        'L0_xattn_bv', 'L0_xattn_Wo', 'L0_xattn_bo', 'L0_ffn_gate', 'L0_ffn_W1', 'L0_ffn_b1', 'L0_ffn_W2', 'L0_ffn_b2',
        'L0_ffn_Ws1', 'L0_ffn_bs1', 'L0_ffn_Ws2', 'L0_ffn_bs2']


def kernel(**inputs):
    import concourse.bacc as _bacc
    from concourse.bass_utils import run_bass_kernel_spmd as _run

    nc = _bacc.Bacc("TRN2", target_bir_lowering=False, num_devices=1)
    arrays, args = {}, []
    for name in _INS:
        a = np.ascontiguousarray(inputs[name])
        if a.dtype == np.bool_:
            a = a.view(np.uint8)
        arrays[name] = a
        args.append(nc.dram_tensor(name, a.shape, mybir.dt.from_np(a.dtype), kind="ExternalInput").ap())
    for name, a in zip(("consts", "kbits"), constants()):
        arrays[name] = a
        args.append(nc.dram_tensor(name, a.shape, mybir.dt.from_np(a.dtype), kind="ExternalInput").ap())
    args.append(nc.dram_tensor("out", (B, S, D), F32, kind="ExternalOutput").ap())
    args.append(nc.dram_tensor("gather_table", (T, ROW), F32).ap())
    args.append(nc.dram_tensor("token_lists", (E * CAP,), I32).ap())
    build(nc, *args)
    r = _run(nc, [arrays], core_ids=[0])
    return r.results[0]["out"]
```

```python
from contextlib import ExitStack

import numpy as np

import concourse.bass as bass
from concourse import mybir

F32 = mybir.dt.float32
BF16 = mybir.dt.bfloat16
F16 = mybir.dt.float16
I32 = mybir.dt.int32
U32 = mybir.dt.uint32
U8 = mybir.dt.uint8
ALU = mybir.AluOpType
ACT = mybir.ActivationFunctionType
AX = mybir.AxisListType

P = 128
B, S, D = 64, 64, 128
H, DH = 16, 8
T = B * S
NT = T // P
UT = 2
NU = NT // UT
E = 8
F = 512
NM = F // P
CAP = T // E
NI = CAP // P
FB = 512
NB = T // FB
EPS = 1e-5
MASKED = 1e30
SCALE = float(DH) ** -0.5
BITS = 30
SEARCH = BITS // 2
NA, NBL = 16, 32
EH = E // 2
NG = 3
ROW = D + E

C_ID, C_J, C_PM, C_STK, C_SAME, C_TRI = 0, 128, 132, 134, 166, 294
C_SEG, C_TOK, C_ST, C_IND = 422, 678, 934, 949
C_END = C_IND + 128
R_B1, R_BS1, R_B2, R_BS2, R_BQ, R_BK, R_BV, R_BO = 0, 32, 36, 44, 45, 46, 47, 48
NR = 49


def constants():
    r = np.arange(P)
    c = np.zeros((P, C_END), np.float32)
    c[:, C_ID:C_ID + P] = np.eye(P)
    c[:, C_J:C_J + 4] = (r[:, None] // DH) % 4 == np.arange(4)
    c[:, C_PM:C_PM + 2] = (r[:, None] // (2 * DH)) % 2 == np.arange(2)
    c[:, C_STK:C_STK + NBL] = r[:, None] % NBL == np.arange(NBL)
    c[:, C_SAME:C_SAME + P] = r[:, None] % E == r % E
    c[:, C_TRI:C_TRI + P] = r[:, None] < r
    c[:, C_SEG:C_SEG + E * NT] = (np.arange(E * NT) % NT) != 0
    c[:, C_TOK:C_TOK + E * NT] = r[:, None] + P * (np.arange(E * NT) % NT) - T // 2
    c[:, C_ST:C_ST + SEARCH] = 2.0 ** (BITS - 2 - 2 * np.arange(SEARCH))
    c[0:2, C_IND:C_IND + P] = np.arange(2)[:, None] == r // 64
    k = (np.arange(1, 4)[None, :] << (BITS - 2 - 2 * np.arange(SEARCH))[:, None]).astype(np.int32)
    return c, np.broadcast_to(k.reshape(1, -1), (P, 3 * SEARCH)).copy()


def build(nc, x, ctx_in, mask, Wq, bq, Wk, bk, Wv, bv, Wo, bo, gate, W1, b1, W2, b2, Ws1, bs1, Ws2, bs2,
          consts, kbits, out, table, lists):
    es = ExitStack()
    with es:
        def sb(name, shape, dt=F32):
            return es.enter_context(nc.sbuf_tensor(name, shape, dt))

        def sem(name):
            return es.enter_context(nc.semaphore(name))

        cst = sb("cst", [P, C_END])
        kb = sb("kb", [P, SEARCH, 3], I32)
        ident = cst[:, C_ID:C_ID + P]
        bias_rows = sb("bias_rows", [NR, P])
        bias_c = sb("bias_c", [P, NR])
        bo2 = sb("bo2", [P, 1])
        wqkv = sb("wqkv", [P, 3, D])
        wo = sb("wo", [P, D])
        wom = sb("wom", [P, 2, D])
        gate_w = sb("gate_w", [P, E])
        mask8 = sb("mask8", [2, NT, S], U8)
        maskr = sb("maskr", [2, NT, S], BF16)
        ind = sb("ind", [2, P], BF16)
        same = sb("same", [P, P], BF16)
        tri = sb("tri", [P, P], BF16)
        ones = sb("ones", [P, P], BF16)
        tokh = sb("tokh", [P, E * NT], F16)
        X = sb("X", [P, NT, D])
        cin = sb("cin", [P, 2, UT, D])
        st1 = sb("st1", [P, 2, UT, 6])
        mv1 = sb("mv1", [P, 2, UT, 2])
        rs1 = sb("rs1", [P, 2, UT])
        st2 = sb("st2", [P, 2, UT, 6])
        mv2 = sb("mv2", [P, 2, UT, 2])
        rs2 = sb("rs2", [P, 2, UT])
        mhalf = sb("mhalf", [P, UT])
        xh1 = sb("xh1", [P, 2, UT, D])
        xcT = sb("xcT", [P, 2, 2 * UT, P])
        QT = sb("QT", [P, 2, UT * P])
        KT = sb("KT", [P, 2, UT * P])
        Kbd = sb("Kbd", [P, 2, 4, UT * P])
        Vz = sb("Vz", [P, 2, 4, D])
        held = sb("held", [P, 2])
        mx = sb("mx", [P, 2, H])
        Pn = sb("Pn", [P, 2, 2, H * S])
        PTs = sb("PTs", [P, 2, 8, P])
        sums = sb("sums", [P, 2, H])
        rsum = sb("rsum", [P, 2, H])
        OLn = sb("OLn", [P, 2, 4, P])
        yTs = sb("yTs", [P, 2, UT * P])
        xh2 = sb("xh2", [P, 2, UT, D])
        x2Ts = sb("x2Ts", [P, 2, UT * P])
        X2T = sb("X2T", [P, T])
        lg = sb("lg", [P, NT, E])
        mxl = sb("mxl", [P, NT])
        pe_ = sb("pe_", [P, NT, E])
        sml = sb("sml", [P, NT])
        rsl = sb("rsl", [P, NT])
        pr8 = sb("pr8", [P, NT, E])
        prT = sb("prT", [P, 2 * P])
        cand = sb("cand", [P, 3], I32)
        cur = sb("cur", [P, 1], I32)
        junk = sb("junk", [P, 3, 2 * P], BF16)
        cnt = sb("cnt", [P, 3], BF16)
        junk3 = sb("junk3", [P, 3])
        nf = sb("nf", [P, 1])
        stepi = sb("stepi", [P, 1], I32)
        thr_b = sb("thr_b", [P, P])
        thr = sb("thr", [P, E])
        gtm = sb("gtm", [P, E, NT], BF16)
        eqm = sb("eqm", [P, E, NT], BF16)
        selm = sb("selm", [P, E, NT], BF16)
        scn = sb("scn", [P, E, NT])
        rk = sb("rk", [P, E, NT])
        rk2 = sb("rk2", [P, E, NT])
        gcn = sb("gcn", [P, E])
        need = sb("need", [P, E])
        posi = sb("posi", [P, E * NT], I32)
        pa = sb("pa", [P, E * NT], I32)
        pb = sb("pb", [P, E * NT], I32)
        pab = sb("pab", [P, E * NT], F16)
        pbb = sb("pbb", [P, E * NT], F16)
        Awt = sb("Awt", [P, NA, E * NT], F16)
        Boh = sb("Boh", [P, NBL, E * NT], F16)
        tokp = sb("tokp", [P, E, NA])
        idx = sb("idx", [P, E, NI], U32)
        ws1 = sb("ws1", [P, F])
        ws2 = sb("ws2", [P, NM, D])
        w1 = sb("w1", [P, E, F])
        w2 = sb("w2", [P, E, NM, D])
        hT = sb("hT", [P, NM, FB])
        yT = sb("yT", [P, FB])
        yo = sb("yo", [P, 2, NI, D])
        gx = sb("gx", [P, NG, NI, ROW])
        xeT = sb("xeT", [P, 2, CAP])

        psS = es.enter_context(nc.psum_tensor("psS", [P, 4, 512], F32))
        psT = es.enter_context(nc.psum_tensor("psT", [P, 2, 512], F32))
        psO = es.enter_context(nc.psum_tensor("psO", [P, 512], F32))
        psJ = es.enter_context(nc.psum_tensor("psJ", [P, 512], F32))

        names = """c_ld br_ld w_ld m_ld wf_ld x_ld0 x_ld1 x_ld2 x_ld3 ctx_ld0 ctx_ld1 tab_st0 tab_st1
            pe_bias bias_ok bo2_mm bo2_ok cdve cpool mrow
            v_st1 v_ag1 v_ve1 pl_rs1 v_xh1 v_max v_sub v_sum v_rec a_o pl_pn v_x1 v_st2 v_ag2 v_ve2 pl_rs2 v_xh2
            v_gate v_v a_xt a_q a_k a_v a_exp a_pt a_y pl_x2 a_x2t pl_kbd
            t_xt t_qk t_v t_S0 t_S t_T t_O t_y t_yt t_x2t t_g
            r_step r_p r_prT r_tT r_prs p_st s_cnt s_tot s_upd s_fin t_thr r_m r_ranks r_m2 r_ranks2 r_pos
            w_tok b_oh t_list r_tok t_idx l_ld
            t_h a_h t_yy a_yy t_yo a_ys pl_ys v_yo o_st0 o_st1 g_ld0 g_ld1 g_ld2 t_xe a_xe we_ld sc_st0 sc_st1""".split()
        q = {n: sem(n) for n in names}
        x_ld = [q[f"x_ld{k}"] for k in range(4)]
        ctx_ld = [q["ctx_ld0"], q["ctx_ld1"]]
        tab_st = [q["tab_st0"], q["tab_st1"]]
        g_ld = [q[f"g_ld{k}"] for k in range(NG)]
        o_st = [q["o_st0"], q["o_st1"]]
        sc_st = [q["sc_st0"], q["sc_st1"]]

        x_v = x.rearrange("a s d -> (a s) d").rearrange("(c p) d -> p c d", p=P)
        ctx_v = ctx_in.rearrange("a s d -> (a s) d").rearrange("(c p) d -> p c d", p=P)
        out_rows = out.rearrange("a s d -> (a s) d")
        out_v = out_rows.rearrange("(c p) d -> p c d", p=P)
        tab_v = table.rearrange("(c p) w -> p c w", p=P)

        FIRST, LAST = -2, NU + 3
        LOOP0, NLOOP = 4, (NU - 3 - 4) // 2

        class Step:

            def __init__(self, i, u0, looped):
                self.i, self.u0, self.looped = i, u0, looped

            def u(self, k):
                return 2 * self.i + (self.u0 + k) if self.looped else self.u0 + k

            def half(self, k):
                return self.i + (self.u0 + k) // 2 if self.looped else (self.u0 + k) // 2

            def par(self, k):
                return (self.u0 + k) % 2

            def on(self, k):
                return self.looped or 0 <= self.u0 + k < NU

        def pipeline(eng, body):
            for u in range(FIRST, LOOP0):
                body(Step(0, u, False))
            with eng.Fori(0, NLOOP) as i:
                body(Step(i, LOOP0, True))
                body(Step(i, LOOP0 + 1, True))
            for u in range(LOOP0 + 2 * NLOOP, LAST):
                body(Step(0, u, False))

        FILL = {(NU + 1, "y"): [(0, 0)], (NU + 1, "yt"): [(0, 1)], (NU + 1, "x2t"): [(0, 2)],
                (NU + 1, "g"): [(0, 3), (1, 0), (1, 1)], (NU + 2, "g"): [(1, 2), (1, 3)]}

        def fill(s, stage, quarter):
            if not s.looped:
                for n, m in FILL.get((s.u0, stage), []):
                    quarter(n, m)

        def wait(eng, s, value):
            if not isinstance(value, int) or value > 0:
                eng.wait_ge(q[s] if isinstance(s, str) else s, value)

        def half(h):
            return slice(EH * NT * h, EH * NT * (h + 1))

        block = es.enter_context(nc.Block())

        @block.sync
        def _(sp):
            sp.dma_start(cst[:], consts).then_inc(q["c_ld"], 16)
            for k in range(4):
                sp.dma_start(X[:, 8 * k:8 * k + 8, :], x_v[:, 8 * k:8 * k + 8, :]).then_inc(x_ld[k], 16)
                if k == 0:
                    for p in range(2):
                        sp.dma_start(cin[:, p], ctx_v[:, UT * p:UT * p + UT, :]).then_inc(ctx_ld[p], 16)

            def body(s):
                if s.on(3) and (s.looped or s.u0 + 3 >= 2):
                    wait(sp, "t_xt", s.u(2))
                    sp.dma_start(cin[:, s.par(3)], ctx_v[:, bass.ds(UT * s.u(3), UT), :]).then_inc(
                        ctx_ld[s.par(3)], 16)
                if s.on(-2):
                    wait(sp, "v_xh2", s.u(-1))
                    sp.dma_start(tab_v[:, bass.ds(UT * s.u(-2), UT), 0:D], xh2[:, s.par(-2)]).then_inc(
                        tab_st[s.par(-2)], 16)

            pipeline(sp, body)
            sp.dma_start(w1[:], W1.rearrange("e p f -> p e f")).then_inc(q["we_ld"], 16)
            for e in range(E):
                sp.dma_start(w2[:, e], W2[e].rearrange("(m p) d -> p m d", p=P)).then_inc(q["we_ld"], 16)
            sp.wait_ge(q["r_p"], 1)
            sp.dma_start(tab_v[:, :, D:ROW], pr8[:]).then_inc(q["p_st"], 16)
            for b in range(NB):
                sp.wait_ge(q["pl_ys"], b + 1)
                sp.dma_start(out_v[:, NI * b:NI * b + NI, :], yo[:, b % 2]).then_inc(o_st[b % 2], 16)
            for p in range(2):
                sp.wait_ge(o_st[p], 16 * (NB // 2))

        def y_evac(act, n):
            act.wait_ge(q["t_yy"], NM * (n + 1))
            wait(act, "t_yo", n)
            b = R_BS2 if n < NB else R_B2 + n - NB
            nc.scalar.activation(yT[:], psO[:], ACT.Identity, bias=bias_c[:, b:b + 1]).then_inc(q["a_yy"], 1)

        @block.scalar
        def _(act):
            act.dma_start(bias_rows[R_B1:R_B1 + E * NM, :], b1.rearrange("e (m p) -> (e m) p", p=P)).then_inc(q["br_ld"], 16)
            act.dma_start(bias_rows[R_BS1:R_BS1 + NM, :], bs1.rearrange("(m p) -> m p", p=P)).then_inc(q["br_ld"], 16)
            act.dma_start(bias_rows[R_B2:R_B2 + E, :], b2).then_inc(q["br_ld"], 16)
            for r, v in ((R_BS2, bs2), (R_BQ, bq), (R_BK, bk), (R_BV, bv), (R_BO, bo)):
                act.dma_start(bias_rows[r:r + 1, :], v.rearrange("(a d) -> a d", a=1)).then_inc(q["br_ld"], 16)
            for k, w in enumerate((Wq, Wk, Wv)):
                act.dma_start(wqkv[:, k, :], w).then_inc(q["w_ld"], 16)
            act.dma_start(wo[:], Wo).then_inc(q["w_ld"], 16)
            act.dma_start(gate_w[:], gate).then_inc(q["w_ld"], 16)
            act.dma_start(mask8[:], mask.rearrange("(i b) k -> b i k", b=2)).then_inc(q["m_ld"], 16)
            act.dma_start(kb[:], kbits.rearrange("p (s k) -> p s k", k=3)).then_inc(q["m_ld"], 16)
            act.dma_start(ws1[:], Ws1).then_inc(q["wf_ld"], 16)
            act.dma_start(ws2[:], Ws2.rearrange("(m p) d -> p m d", p=P)).then_inc(q["wf_ld"], 16)
            act.wait_ge(q["pe_bias"], 1)
            nc.scalar.copy(bias_c[:], psJ[:, 0:NR]).then_inc(q["bias_ok"], 1)
            act.wait_ge(q["bo2_mm"], 1)
            act.wait_ge(q["bias_ok"], 1)
            nc.scalar.activation(bo2[:], psJ[:, 0:1], ACT.Identity, bias=bias_c[:, R_BO:R_BO + 1]).then_inc(q["bo2_ok"], 1)

            def hidden_out(n, m):
                if m == 2 and n > 0 and n != NB:
                    y_evac(act, n - 1)
                act.wait_ge(q["t_h"], NM * n + m + 1)
                wait(act, "t_yy", NM * (n - 1) + m + 1)
                b = R_BS1 + m if n < NB else R_B1 + NM * (n - NB) + m
                nc.scalar.activation(hT[:, m], psS[:, m], ACT.Gelu_apprx_tanh, bias=bias_c[:, b:b + 1]).then_inc(q["a_h"], 1)
                if m == 2 and 0 < n < NB:
                    shared_out(n - 1)

            def shared_out(b):
                act.wait_ge(q["t_yo"], b + 1)
                if b >= 2:
                    act.wait_ge(o_st[b % 2], 16 * (b // 2))
                nc.scalar.copy(yo[:, b % 2], psT[:, 0].rearrange("p (a d) -> p a d", a=NI)).then_inc(q["a_ys"], 1)

            def pt_evac(s, k, pr, hf):
                wait(act, "t_T", 4 * s.u(k) + 2 * pr + hf + 1)
                wait(act, "t_O", 2 * s.u(k) + pr - 1)
                nc.scalar.copy(PTs[:, pr, 4 * hf:4 * hf + 4, :], psT[:, hf].rearrange("p (a t) -> p a t", a=4)).then_inc(q["a_pt"], 1)

            def exps(s, pr):
                wait(act, "v_sub", 2 * s.u(0) + pr + 1)
                nc.scalar.activation(Pn[:, s.par(0), pr], Pn[:, s.par(0), pr], ACT.Exp, scale=SCALE).then_inc(q["a_exp"], 1)

            def body(s):
                if s.on(-2):
                    wait(act, "t_y", s.u(-1))
                    wait(act, "t_yt", s.u(-3))
                    nc.scalar.activation(yTs[:, s.par(-2)], psJ[:, 0:UT * P], ACT.Identity, bias=bo2[:, 0:1]).then_inc(q["a_y"], 1)
                fill(s, "y", hidden_out)
                fill(s, "yt", hidden_out)
                if s.on(1):
                    wait(act, "t_xt", s.u(2))
                    wait(act, "t_v", s.u(0))
                    nc.scalar.copy(xcT[:, s.par(1)], psJ.rearrange("p (a t) -> p a t", a=4)).then_inc(q["a_xt"], 1)
                if s.on(0):
                    exps(s, 0)
                if s.on(-1):
                    pt_evac(s, -1, 0, 0)
                    pt_evac(s, -1, 0, 1)
                if s.on(1):
                    wait(act, "t_qk", s.u(2))
                    wait(act, "t_S", 2 * s.u(0))
                    wait(act, "pl_kbd", s.u(0))
                    nc.scalar.activation(KT[:, s.par(1)], psJ[:, UT * P:2 * UT * P], ACT.Identity, bias=bias_c[:, R_BK:R_BK + 1]).then_inc(q["a_k"], 1)
                    nc.scalar.activation(QT[:, s.par(1)], psJ[:, 0:UT * P], ACT.Identity, bias=bias_c[:, R_BQ:R_BQ + 1]).then_inc(q["a_q"], 1)
                if s.on(-3):
                    wait(act, "t_x2t", s.u(-2))
                    wait(act, "t_g", s.u(-4))
                    wait(act, "pl_x2", s.u(-4))
                    nc.scalar.copy(x2Ts[:, s.par(-3)], psJ[:, 0:UT * P]).then_inc(q["a_x2t"], 1)
                fill(s, "x2t", hidden_out)
                fill(s, "g", hidden_out)
                if s.on(-1):
                    pt_evac(s, -1, 1, 0)
                    pt_evac(s, -1, 1, 1)
                if s.on(0):
                    exps(s, 1)
                if s.on(1):
                    wait(act, "t_v", s.u(2))
                    wait(act, "t_O", 2 * s.u(0))
                    v = psJ[0:64, :].rearrange("p (b g h d) -> p b g h d", b=4, h=2, d=DH)
                    o = Vz[0:64, s.par(1)].rearrange("p b (g h d) -> p b g h d", h=2, d=DH)
                    nc.scalar.copy(o[:, :, :, 0, :], v[:, :, :, 0, :]).then_inc(q["a_v"], 1)
                if s.on(-1):
                    wait(act, "t_O", 2 * s.u(0))
                    wait(act, "t_y", s.u(-2))
                    nc.scalar.copy(OLn[:, s.par(-1)], psO.rearrange("p (b t) -> p b t", b=4)).then_inc(q["a_o"], 1)

            act.wait_ge(q["cpool"], 2)
            pipeline(act, body)

            act.wait_ge(q["r_step"], 2)
            nc.scalar.activation(pe_[:], pe_[:], ACT.Exp).then_inc(q["r_prs"], 1)

            for n in range(2, NB + E):
                e = n - NB
                if e == 0:
                    y_evac(act, n - 1)
                    shared_out(n - 1)
                if e >= 0:
                    act.wait_ge(q["t_xe"], e + 1)
                    wait(act, "t_h", NM * (n - 1))
                    nc.scalar.copy(xeT[:, e % 2], psT[:, 1]).then_inc(q["a_xe"], 1)
                for m in range(NM):
                    hidden_out(n, m)
            y_evac(act, NB + E - 1)

        @block.gpsimd
        def _(pool):
            nc.gpsimd.memset(mhalf[:], -0.5).then_inc(q["cpool"], 1)
            nc.gpsimd.memset(Vz[:], 0.0).then_inc(q["cpool"], 1)
            pool.wait_ge(q["c_ld"], 16)

            def normalise(s, pr):
                wait(pool, "v_rec", 2 * s.u(0) + pr + 1)
                pn = Pn[:, s.par(0), pr].rearrange("p (h k) -> p h k", k=S)
                nc.gpsimd.tensor_tensor(pn, pn, rsum[:, pr].unsqueeze(2).to_broadcast([P, H, S]), ALU.mult).then_inc(q["pl_pn"], 1)

            def body(s):
                if s.on(1):
                    wait(pool, "a_k", s.u(2))
                    wait(pool, "t_S", 2 * s.u(0))
                    nc.gpsimd.tensor_tensor(
                        Kbd[:, s.par(1)],
                        KT[:, s.par(1)].unsqueeze(1).to_broadcast([P, 4, UT * P]),
                        cst[:, C_J:C_J + 4].unsqueeze(2).to_broadcast([P, 4, UT * P]), ALU.mult).then_inc(q["pl_kbd"], 1)
                if s.on(-2):
                    wait(pool, "v_ve2", s.u(-1))
                    wait(pool, "v_xh2", s.u(-3))
                    nc.gpsimd.tensor_tensor(rs2[:, s.par(-2)], mv2[:, s.par(-2), :, 1], mhalf[:], ALU.pow).then_inc(q["pl_rs2"], 1)
                if s.on(2):
                    wait(pool, "v_ve1", s.u(3))
                    wait(pool, "v_xh1", s.u(1))
                    nc.gpsimd.tensor_tensor(rs1[:, s.par(2)], mv1[:, s.par(2), :, 1], mhalf[:], ALU.pow).then_inc(q["pl_rs1"], 1)
                if s.on(-3):
                    wait(pool, "a_x2t", s.u(-2))
                    nc.gpsimd.tensor_copy(X2T[:, bass.ds(UT * P * s.u(-3), UT * P)], x2Ts[:, s.par(-3)]).then_inc(q["pl_x2"], 1)
                if s.on(0):
                    normalise(s, 0)
                if s.on(0):
                    normalise(s, 1)

            pool.wait_ge(q["cpool"], 2)
            pipeline(pool, body)

            for b in range(NB):
                pool.wait_ge(q["a_ys"], b + 1)
                nc.gpsimd.tensor_tensor(yo[:, b % 2], yo[:, b % 2], X[:, NI * b:NI * b + NI, :], ALU.add).then_inc(q["pl_ys"], 1)
            for p in range(2):
                pool.wait_ge(tab_st[p], 16 * (NU // 2))
            pool.wait_ge(q["p_st"], 16)


            def gather(e):
                if e >= NG:
                    pool.wait_ge(q["v_yo"], e - NG + 1)
                pool.wait_ge(q["l_ld"], e // EH + 1)
                for i in range(NI):
                    pool.indirect_dma_start(
                        out=gx[:, e % NG, i, :], out_offset=None, in_=table[:, :],
                        in_offset=bass.IndirectOffsetOnAxis(ap=idx[:, e, i:i + 1], axis=0)).then_inc(g_ld[e % NG], 16)

            gather(0)
            gather(1)
            gather(2)
            for p in range(2):
                pool.wait_ge(o_st[p], 16 * (NB // 2))
            for e in range(E):
                pool.wait_ge(q["v_yo"], e + 1)
                if e:
                    pool.wait_ge(sc_st[(e - 1) % 2], 16 * NI * ((e - 1) // 2 + 1))
                for i in range(NI):
                    pool.indirect_dma_start(
                        out=out_rows, out_offset=bass.IndirectOffsetOnAxis(ap=idx[:, e, i:i + 1], axis=0),
                        in_=yo[:, e % 2, i, :], in_offset=None, compute_op=ALU.add).then_inc(sc_st[e % 2], 16)
                if e + 3 < E:
                    gather(e + 3)
            for p in range(2):
                pool.wait_ge(sc_st[p], 16 * NI * (E // 2))

        @block.vector
        def _(dve):
            dve.wait_ge(q["c_ld"], 16)
            nc.vector.tensor_copy(ind[:], cst[0:2, C_IND:C_IND + P]).then_inc(q["cdve"], 1)
            nc.vector.tensor_copy(same[:], cst[:, C_SAME:C_SAME + P]).then_inc(q["cdve"], 1)
            nc.vector.tensor_copy(tri[:], cst[:, C_TRI:C_TRI + P]).then_inc(q["cdve"], 1)
            nc.vector.memset(ones[:], 1.0).then_inc(q["cdve"], 1)
            nc.vector.tensor_copy(tokh[:], cst[:, C_TOK:C_TOK + E * NT]).then_inc(q["cdve"], 1)
            dve.wait_ge(q["w_ld"], 16 * 5)
            for k in range(2):
                nc.vector.tensor_scalar(wom[:, k], wo[:], cst[:, C_PM + k:C_PM + k + 1], None, ALU.mult).then_inc(q["cdve"], 1)
            dve.wait_ge(q["m_ld"], 32)
            nc.vector.tensor_scalar(maskr[:], mask8[:], 1.0, MASKED, ALU.subtract, ALU.mult).then_inc(q["mrow"], 1)
            for k in range(4):
                dve.wait_ge(x_ld[k], 16)

            def stats(v, par, c0, st, mv, n_st, n_ag, n_ve):
                nc.vector.memset(held[:, 0:1], 0.0)
                for t in range(UT):
                    nc.vector.bn_stats(st[:, par, t], X[:, bass.ds(c0 + t, 1), :].rearrange("p a d -> p (a d)")).then_inc(q[n_st], 1)
                wait(dve, n_st, UT * (v + 1))
                nc.vector.memset(held[:, 1:2], 0.0)
                for t in range(UT):
                    nc.vector.bn_aggr(mv[:, par, t], st[:, par, t]).then_inc(q[n_ag], 1)
                wait(dve, n_ag, UT * (v + 1))
                nc.vector.tensor_scalar(mv[:, par, :, 1], mv[:, par, :, 1], EPS, None, ALU.add).then_inc(q[n_ve], 1)

            def normed(dst, par, c0, mv, rs, name):
                for t in range(UT):
                    ins = nc.vector.tensor_scalar(dst[:, par, t], X[:, bass.ds(c0 + t, 1), :].rearrange("p a d -> p (a d)"),
                                                  mv[:, par, t, 0:1], rs[:, par, t:t + 1], ALU.subtract, ALU.mult)
                ins.then_inc(q[name], 1)

            def centre(s, pr):
                wait(dve, "t_S", 2 * s.u(0) + pr + 1)
                z = psS[:, 2 * pr:2 * pr + 2, :].rearrange("p a (h k) -> p (a h) k", k=S)
                nc.vector.tensor_reduce(mx[:, pr], z, AX.X, ALU.max).then_inc(q["v_max"], 1)
                wait(dve, "v_max", 2 * s.u(0) + pr + 1)
                wait(dve, "t_T", 4 * s.u(-2) + 2 * pr + 2)
                nc.vector.tensor_tensor(Pn[:, s.par(0), pr].rearrange("p (h k) -> p h k", k=S), z,
                                        mx[:, pr].unsqueeze(2).to_broadcast([P, H, S]), ALU.subtract).then_inc(q["v_sub"], 1)

            def row_sums(s, pr):
                n = 2 * s.u(0) + pr + 1
                wait(dve, "a_exp", n)
                nc.vector.tensor_reduce(sums[:, pr], Pn[:, s.par(0), pr].rearrange("p (h k) -> p h k", k=S), AX.X, ALU.add).then_inc(q["v_sum"], 1)
                wait(dve, "v_sum", n)
                wait(dve, "pl_pn", n - 2)
                nc.vector.reciprocal(rsum[:, pr], sums[:, pr]).then_inc(q["v_rec"], 1)

            def body(s):
                if s.on(-2):
                    wait(dve, "t_yt", s.u(-1))
                    xs = X[:, bass.ds(UT * s.u(-2), UT), :].rearrange("p a d -> p (a d)")
                    nc.vector.tensor_tensor(xs, xs, psJ[:, 0:UT * P], ALU.add).then_inc(q["v_x1"], 1)
                if s.on(0):
                    centre(s, 0)
                    centre(s, 1)
                if s.on(-2):
                    wait(dve, "v_x1", s.u(-1))
                    stats(s.u(-2), s.par(-2), UT * s.u(-2), st2, mv2, "v_st2", "v_ag2", "v_ve2")
                if s.on(2):
                    stats(s.u(2), s.par(2), UT * s.u(2), st1, mv1, "v_st1", "v_ag1", "v_ve1")
                if s.on(0):
                    row_sums(s, 0)
                if s.on(1):
                    wait(dve, "t_v", s.u(2))
                    wait(dve, "t_O", 2 * s.u(0))
                    v = psJ[64:128, :].rearrange("p (b g h d) -> p b g h d", b=4, h=2, d=DH)
                    o = Vz[64:128, s.par(1)].rearrange("p b (g h d) -> p b g h d", h=2, d=DH)
                    nc.vector.tensor_copy(o[:, :, :, 1, :], v[:, :, :, 1, :]).then_inc(q["v_v"], 1)
                if s.on(0):
                    row_sums(s, 1)
                if s.on(-3):
                    wait(dve, "t_g", s.u(-2))
                    nc.vector.tensor_copy(lg[:, bass.ds(UT * s.u(-3), UT), :].rearrange("p a e -> p (a e)"), psT[:, 0, 0:UT * E]).then_inc(q["v_gate"], 1)
                if s.on(-2):
                    wait(dve, "pl_rs2", s.u(-1))
                    wait(dve, "t_x2t", s.u(-3))
                    wait(dve, tab_st[s.par(-2)], 16 * s.half(-2))
                    normed(xh2, s.par(-2), UT * s.u(-2), mv2, rs2, "v_xh2")
                if s.on(2):
                    wait(dve, "pl_rs1", s.u(3))
                    wait(dve, "t_xt", s.u(1))
                    normed(xh1, s.par(2), UT * s.u(2), mv1, rs1, "v_xh1")

            dve.wait_ge(q["cpool"], 2)
            pipeline(dve, body)

            dve.wait_ge(q["v_gate"], NU)
            nc.vector.tensor_reduce(mxl[:], lg[:], AX.X, ALU.max).then_inc(q["r_step"], 1)
            dve.wait_ge(q["r_step"], 1)
            nc.vector.tensor_tensor(pe_[:], lg[:], mxl[:].unsqueeze(2).to_broadcast([P, NT, E]), ALU.subtract).then_inc(q["r_step"], 1)
            dve.wait_ge(q["r_prs"], 1)
            nc.vector.tensor_reduce(sml[:], pe_[:], AX.X, ALU.add).then_inc(q["r_step"], 1)
            dve.wait_ge(q["r_step"], 3)
            nc.vector.reciprocal(rsl[:], sml[:]).then_inc(q["r_step"], 1)
            dve.wait_ge(q["r_step"], 4)
            nc.vector.tensor_tensor(pr8[:], pe_[:], rsl[:].unsqueeze(2).to_broadcast([P, NT, E]), ALU.mult).then_inc(q["r_p"], 1)
            dve.wait_ge(q["r_tT"], 1)
            nc.vector.tensor_copy(prT[:], psT[:, 1, 0:2 * P]).then_inc(q["r_prT"], 1)
            nc.vector.memset(cur[:], 0).then_inc(q["s_upd"], 1)
            nc.vector.tensor_copy(cand[:], kb[:, 0]).then_inc(q["s_upd"], 1)
            dve.wait_ge(q["r_prT"], 1)

            for k in range(SEARCH):
                dve.wait_ge(q["s_upd"], 2 + 4 * k)
                if k:
                    dve.wait_ge(q["s_tot"], k)
                for j in range(3):
                    with nc.allow_low_precision(reason="counts up to 256 are exact"):
                        ins = nc.vector.tensor_scalar(junk[:, j], prT[:], cand[:, j:j + 1].bitcast(F32), 0.0, ALU.is_ge, ALU.add,
                                                      accum_out=cnt[:, j:j + 1])
                    ins.then_inc(q["s_cnt"], 1)
                dve.wait_ge(q["s_tot"], k + 1)
                nc.vector.tensor_scalar(junk3[:], psT[:, 1, 0:3], float(CAP), 0.0, ALU.is_ge, ALU.add,
                                        accum_out=nf[:]).then_inc(q["s_upd"], 1)
                dve.wait_ge(q["s_upd"], 2 + 4 * k + 1)
                nc.vector.tensor_scalar(stepi[:], nf[:], cst[:, C_ST + k:C_ST + k + 1], None, ALU.mult).then_inc(q["s_upd"], 1)
                dve.wait_ge(q["s_upd"], 2 + 4 * k + 2)
                nc.vector.tensor_tensor(cur[:], cur[:], stepi[:], ALU.bitwise_or).then_inc(q["s_upd"], 1)
                dve.wait_ge(q["s_upd"], 2 + 4 * k + 3)
                if k + 1 < SEARCH:
                    nc.vector.tensor_tensor(cand[:], kb[:, k + 1], cur[:].to_broadcast([P, 3]), ALU.bitwise_or).then_inc(q["s_upd"], 1)
            nc.vector.tensor_copy(thr_b[:], cur[:].bitcast(F32).to_broadcast([P, P])).then_inc(q["s_fin"], 1)
            dve.wait_ge(q["t_thr"], 1)
            nc.vector.tensor_copy(thr[:], psT[:, 1, 0:E]).then_inc(q["s_fin"], 1)
            dve.wait_ge(q["s_fin"], 2)
            tb = thr[:].unsqueeze(1).to_broadcast([P, NT, E])
            nc.vector.tensor_tensor(gtm[:].rearrange("p e c -> p c e"), pr8[:], tb, ALU.is_gt).then_inc(q["r_m"], 1)
            nc.vector.tensor_tensor(eqm[:].rearrange("p e c -> p c e"), pr8[:], tb, ALU.is_equal).then_inc(q["r_m"], 1)

            def ranks(name, tri_tot):
                before, tot = psJ[:, 0:E * NT], psJ[:, E * NT:2 * E * NT]
                nc.vector.tensor_tensor_scan(scn[:].rearrange("p e c -> p (e c)"), cst[:, C_SEG:C_SEG + E * NT], tot, 0.0,
                                             ALU.mult, ALU.add).then_inc(q[name], 1)
                dve.wait_ge(q[name], 1)
                nc.vector.tensor_tensor(rk[:].rearrange("p e c -> p (e c)"), scn[:].rearrange("p e c -> p (e c)"), before, ALU.add).then_inc(q[name], 1)
                dve.wait_ge(q[name], 2)
                nc.vector.tensor_tensor(rk2[:].rearrange("p e c -> p (e c)"), rk[:].rearrange("p e c -> p (e c)"), tot, ALU.subtract).then_inc(q[name], 1)
                dve.wait_ge(q[name], 3)

            dve.wait_ge(q["r_ranks"], 1)
            ranks("r_m2", None)
            nc.vector.tensor_reduce(gcn[:], psT[:, 1, 0:E * NT].rearrange("p (e c) -> p e c", e=E), AX.X, ALU.add).then_inc(q["r_m2"], 1)
            dve.wait_ge(q["r_m2"], 4)
            nc.vector.tensor_scalar(need[:], gcn[:], -1.0, float(CAP), ALU.mult, ALU.add).then_inc(q["r_m2"], 1)
            dve.wait_ge(q["r_m2"], 5)
            nc.vector.tensor_tensor(rk[:], rk2[:], need[:].unsqueeze(2).to_broadcast([P, E, NT]), ALU.is_lt).then_inc(q["r_m2"], 1)
            dve.wait_ge(q["r_m2"], 6)
            nc.vector.tensor_tensor(rk2[:], rk[:], eqm[:], ALU.mult).then_inc(q["r_m2"], 1)
            dve.wait_ge(q["r_m2"], 7)
            nc.vector.tensor_tensor(selm[:], rk2[:], gtm[:], ALU.add).then_inc(q["r_m"], 1)
            dve.wait_ge(q["r_ranks"], 2)
            dve.wait_ge(q["r_m"], 3)
            ranks("r_ranks2", None)
            nc.vector.tensor_scalar(rk[:], selm[:], -2.0 * CAP, 2.0 * CAP, ALU.mult, ALU.add).then_inc(q["r_ranks2"], 1)
            dve.wait_ge(q["r_ranks2"], 4)
            nc.vector.tensor_tensor(posi[:], rk[:].rearrange("p e c -> p (e c)"), rk2[:].rearrange("p e c -> p (e c)"), ALU.add).then_inc(q["r_ranks2"], 1)
            dve.wait_ge(q["r_ranks2"], 5)
            nc.vector.tensor_scalar(pa[:], posi[:], 5, None, ALU.logical_shift_right).then_inc(q["r_ranks2"], 1)
            nc.vector.tensor_scalar(pb[:], posi[:], NBL - 1, None, ALU.bitwise_and).then_inc(q["r_ranks2"], 1)
            dve.wait_ge(q["r_ranks2"], 6)
            nc.vector.tensor_copy(pab[:], pa[:]).then_inc(q["r_pos"], 1)
            dve.wait_ge(q["r_ranks2"], 7)
            nc.vector.tensor_copy(pbb[:], pb[:]).then_inc(q["r_pos"], 1)
            dve.wait_ge(q["r_pos"], 2)

            def one_hot_low(h):
                for i in range(NBL):
                    ins = nc.vector.tensor_scalar(Boh[:, i, half(h)], pbb[:, half(h)], float(i), None, ALU.is_equal)
                ins.then_inc(q["b_oh"], 1)

            def one_hot_high(h, i0, i1):
                for i in range(i0, i1):
                    nc.vector.scalar_tensor_tensor(out=Awt[:, i, half(h)], in0=pab[:, half(h)], scalar=float(i), in1=tokh[:, half(h)],
                                                   op0=ALU.is_equal, op1=ALU.mult).then_inc(q["w_tok"], 1)

            def list_parts(h):
                dve.wait_ge(q["t_list"], h + 1)
                nc.vector.tensor_copy(tokp[:, EH * h:EH * (h + 1)], psJ[:, EH * NA * h:EH * NA * (h + 1)].rearrange("p (e a) -> p e a", e=EH)).then_inc(q["r_tok"], 1)

            def list_out(h):
                dve.wait_ge(q["t_idx"], h + 1)
                nc.vector.tensor_scalar(idx[:, EH * h:EH * (h + 1)], psT[:, 1, 0:EH * NI].rearrange("p (e i) -> p e i", e=EH),
                                        float(T // 2), None, ALU.add).then_inc(q["l_ld"], 1)

            one_hot_low(0)
            one_hot_high(0, 0, NA)
            one_hot_low(1)
            list_parts(0)
            one_hot_high(1, 0, 4)
            list_out(0)
            one_hot_high(1, 4, NA)
            list_parts(1)
            list_out(1)
            for e in range(E):
                dve.wait_ge(q["t_yo"], NB + e + 1)
                dve.wait_ge(g_ld[e % NG], 16 * NI * (e // NG + 1))
                if e < 2:
                    dve.wait_ge(o_st[e % 2], 16 * (NB // 2))
                else:
                    dve.wait_ge(sc_st[e % 2], 16 * NI * (e // 2))
                nc.vector.tensor_tensor(yo[:, e % 2], psT[:, 0].rearrange("p (a d) -> p a d", a=NI),
                                        gx[:, e % NG, :, D + e:D + e + 1].to_broadcast([P, NI, D]), ALU.mult).then_inc(q["v_yo"], 1)

        @block.tensor
        def _(pe):
            mm, tr = nc.tensor.matmul, nc.tensor.transpose
            pe.wait_ge(q["c_ld"], 16)
            pe.wait_ge(q["br_ld"], 16 * 8)
            tr(psJ[:, 0:NR], bias_rows[:], ident[0:NR, 0:NR]).then_inc(q["pe_bias"], 1)
            pe.wait_ge(q["bias_ok"], 1)
            pe.wait_ge(q["w_ld"], 16 * 5)
            mm(psJ[:, 0:1], wo[:], bias_c[:, R_BV:R_BV + 1], start=True, stop=True).then_inc(q["bo2_mm"], 1)
            pe.wait_ge(q["bo2_ok"], 1)
            pe.wait_ge(q["cdve"], 7)
            pe.wait_ge(q["mrow"], 1)

            def logits_even(s, pr):
                wait(pe, "v_sub", 2 * s.u(-1) + pr + 1)
                for bank in range(2):
                    m = maskr[:, bass.ds(UT * s.u(0) + pr, 1), :].to_broadcast([2, 8, S])
                    mm(psS[:, 2 * pr + bank], ind[:], m, start=True, stop=False, skip_group_check=True)
                logits_of(s, pr, (0, 2), False).then_inc(q["t_S0"], 1)

            def logits_odd(s, pr):
                wait(pe, "t_S0", 2 * s.u(0) + pr + 1)
                logits_of(s, pr, (1, 3), True).then_inc(q["t_S"], 1)

            def logits_of(s, pr, groups, stop):
                p = s.par(0)
                for g in groups:
                    for b in range(2):
                        r, c = 32 * g, P * pr + 64 * b
                        ins = mm(psS[64 * b:64 * b + 64, 2 * pr + g // 2, 256 * (g % 2):256 * (g % 2) + 256],
                                 QT[r:r + 32, p, c:c + 64], Kbd[r:r + 32, p, :, c:c + 64], start=False, stop=stop,
                                 tile_position=(r, 64 * b), skip_group_check=True)
                return ins

            def p_transpose(s, pr, hf):
                v = 4 * s.u(-1) + 2 * pr + hf
                wait(pe, "pl_pn", 2 * s.u(-1) + pr + 1)
                wait(pe, "a_pt", v - 1)
                for a in range(4):
                    k = 4 * hf + a
                    ins = tr(psT[:, hf, P * a:P * a + P], Pn[:, s.par(-1), pr, P * k:P * k + P], ident)
                ins.then_inc(q["t_T"], 1)

            def p_v(s, pr):
                wait(pe, "a_pt", 4 * s.u(-1) + 2 * pr + 2)
                wait(pe, "a_v", s.u(0))
                wait(pe, "v_v", s.u(0))
                wait(pe, "a_o", s.u(-1))
                for b in range(2):
                    for t in range(4):
                        o = P * (2 * pr + b)
                        ins = mm(psO[32 * t:32 * t + 32, o:o + P], Vz[:, s.par(-1), 2 * pr + b, 32 * t:32 * t + 32],
                                 PTs[:, pr, 2 * t:2 * t + 2, 64 * b:64 * b + 64], start=True, stop=True,
                                 tile_position=(0, 32 * t), skip_group_check=True)
                ins.then_inc(q["t_O"], 1)

            def hidden(n, m):
                e = n - NB
                if n < NB and m == 0:
                    pe.wait_ge(q["pl_x2"], FB // (UT * P) * (n + 1))
                if n == 0:
                    pe.wait_ge(q["v_sub"], 2 * NU)
                    pe.wait_ge(q["wf_ld"], 32)
                else:
                    pe.wait_ge(q["a_h"], NM * (n - 1) + m + 1)
                if e >= 0 and m == 0:
                    pe.wait_ge(q["a_xe"], e + 1)
                    pe.wait_ge(q["we_ld"], 16 * (1 + E))
                w = ws1[:, P * m:P * m + P] if e < 0 else w1[:, e, P * m:P * m + P]
                src = X2T[:, FB * n:FB * n + FB] if e < 0 else xeT[:, e % 2]
                mm(psS[:, m], w, src, start=True, stop=True).then_inc(q["t_h"], 1)

            def second(n, m):
                pe.wait_ge(q["a_h"], NM * n + m + 1)
                if m == 0:
                    wait(pe, "a_yy", n)
                    if n == 0:
                        pe.wait_ge(q["a_o"], NU)
                w = ws2[:, m] if n < NB else w2[:, n - NB, m]
                mm(psO[:], w, hT[:, m], start=(m == 0), stop=(m == NM - 1)).then_inc(q["t_yy"], 1)

            def turn_back(n):
                pe.wait_ge(q["a_yy"], n + 1)
                if n == 0:
                    pe.wait_ge(q["v_gate"], NU)
                wait(pe, "a_ys", min(n, NB))
                wait(pe, "v_yo", n - NB)
                for i in range(NI):
                    ins = tr(psT[:, 0, P * i:P * i + P], yT[:, P * i:P * i + P], ident)
                ins.then_inc(q["t_yo"], 1)

            def search(k):
                if k == 0:
                    pe.wait_ge(q["r_p"], 1)
                    for h in range(2):
                        ins = tr(psT[:, 1, P * h:P * h + P], pr8[:, 16 * h:16 * h + 16, :].rearrange("p c e -> p (c e)"), ident)
                    ins.then_inc(q["r_tT"], 1)
                    pe.wait_ge(q["r_prT"], 1)
                pe.wait_ge(q["s_cnt"], 3 * (k + 1))
                if k:
                    pe.wait_ge(q["s_upd"], 2 + 4 * (k - 1) + 1)
                mm(psT[:, 1, 0:3], same[:], cnt[:], start=True, stop=True).then_inc(q["s_tot"], 1)

            def quarter(n, m):
                hidden(n, m)
                if n and n != NB:
                    if m < 2:
                        second(n - 1, 2 + m)
                    elif m == 2:
                        turn_back(n - 1)
                if m >= 2:
                    second(n, m - 2)

            def body(s):
                if s.on(0):
                    wait(pe, "a_q", s.u(1))
                    wait(pe, "pl_kbd", s.u(1))
                    logits_even(s, 0)
                    wait(pe, "a_v", s.u(1))
                    wait(pe, "v_v", s.u(1))
                if s.on(-2):
                    if not s.on(0):
                        wait(pe, "a_x2t", s.u(-3))
                    wait(pe, "a_o", s.u(-1))
                    for k in range(2):
                        ins = mm(psJ[:, 0:UT * P], wom[:, k], OLn[:, s.par(-2), :, 64 * k:64 * k + 64], start=(k == 0), stop=(k == 1))
                    ins.then_inc(q["t_y"], 1)
                    fill(s, "y", quarter)
                if s.on(0):
                    logits_odd(s, 0)
                if s.on(-2):
                    wait(pe, "a_y", s.u(-1))
                    for t in range(UT):
                        ins = tr(psJ[:, P * t:P * t + P], yTs[:, s.par(-2), P * t:P * t + P], ident)
                    ins.then_inc(q["t_yt"], 1)
                    fill(s, "yt", quarter)
                if s.on(0):
                    logits_even(s, 1)
                if s.on(1):
                    wait(pe, "v_x1", s.u(-1))
                    wait(pe, "v_xh1", s.u(2))
                    wait(pe, ctx_ld[s.par(1)], 16 * (s.half(1) + 1))
                    for t in range(UT):
                        tr(psJ[:, P * t:P * t + P], xh1[:, s.par(1), t], ident)
                    for t in range(UT):
                        ins = tr(psJ[:, P * (UT + t):P * (UT + t) + P], cin[:, s.par(1), t], ident)
                    ins.then_inc(q["t_xt"], 1)
                if s.on(0):
                    logits_odd(s, 1)
                if s.on(-1):
                    wait(pe, "v_gate", s.u(-3))
                    p_transpose(s, 0, 0)
                    p_transpose(s, 0, 1)
                if s.on(1):
                    wait(pe, "a_xt", s.u(2))
                    for k in range(2):
                        ins = mm(psJ[:, UT * P * k:UT * P * (k + 1)], wqkv[:, k], xcT[:, s.par(1), UT * k:UT * k + UT], start=True, stop=True)
                    ins.then_inc(q["t_qk"], 1)
                if s.on(-1):
                    p_transpose(s, 1, 0)
                    p_transpose(s, 1, 1)
                if s.on(1):
                    wait(pe, "a_q", s.u(2))
                    wait(pe, "a_k", s.u(2))
                elif s.on(-2):
                    wait(pe, "v_x1", s.u(-1))
                if s.on(-3):
                    wait(pe, "v_xh2", s.u(-2))
                    for t in range(UT):
                        ins = tr(psJ[:, P * t:P * t + P], xh2[:, s.par(-3), t], ident)
                    ins.then_inc(q["t_x2t"], 1)
                    fill(s, "x2t", quarter)
                if s.on(-1):
                    p_v(s, 0)
                if s.on(1):
                    wait(pe, "a_x2t", s.u(-2))
                    for b in range(4):
                        cT = xcT[:, s.par(1), UT + b // 2, 64 * (b % 2):64 * (b % 2) + 64]
                        for h in range(2):
                            ins = mm(psJ[64 * h:64 * h + 64, P * b:P * b + P], cT, wqkv[:, 2], start=True, stop=True,
                                     tile_position=(0, 64 * h), skip_group_check=True)
                    ins.then_inc(q["t_v"], 1)
                if s.on(-1):
                    p_v(s, 1)
                if s.on(-3):
                    wait(pe, "a_x2t", s.u(-2))
                    wait(pe, "a_pt", 4 * s.u(0) - 1 if s.on(-1) else 4 * NU)
                    if not s.on(-1):
                        wait(pe, "v_gate", s.u(-3))
                    for t in range(UT):
                        ins = mm(psT[:, 0, E * t:E * t + E], x2Ts[:, s.par(-3), P * t:P * t + P], gate_w[:], start=True, stop=True)
                    ins.then_inc(q["t_g"], 1)
                    fill(s, "g", quarter)

            pipeline(pe, body)

            def gather_in(e):
                pe.wait_ge(g_ld[e % NG], 16 * NI * (e // NG + 1))
                wait(pe, "a_xe", e)
                for i in range(NI):
                    ins = tr(psT[:, 1, P * i:P * i + P], gx[:, e % NG, i, 0:D], ident)
                ins.then_inc(q["t_xe"], 1)

            def block_of(n, slots):
                for m in range(NM):
                    quarter(n, m)
                    slots[m]()

            none = lambda: None
            fl = lambda a: a[:].rearrange("p e c -> p (e c)")

            def thresholds():
                pe.wait_ge(q["s_fin"], 1)
                tr(psT[:, 1, 0:P], thr_b[:], ident).then_inc(q["t_thr"], 1)

            def ranks_equal():
                pe.wait_ge(q["r_m"], 2)
                pe.wait_ge(q["a_x2t"], NU)
                mm(psJ[:, 0:E * NT], tri[:], fl(eqm), start=True, stop=True)
                mm(psJ[:, E * NT:2 * E * NT], ones[:], fl(eqm), start=True, stop=True)
                mm(psT[:, 1, 0:E * NT], ones[:], fl(gtm), start=True, stop=True).then_inc(q["r_ranks"], 1)

            def ranks_chosen():
                pe.wait_ge(q["r_m"], 3)
                mm(psJ[:, 0:E * NT], tri[:], fl(selm), start=True, stop=True)
                mm(psJ[:, E * NT:2 * E * NT], ones[:], fl(selm), start=True, stop=True).then_inc(q["r_ranks"], 1)

            def token_lists(h):
                pe.wait_ge(q["b_oh"], h + 1)
                pe.wait_ge(q["w_tok"], NA * (h + 1))
                pe.wait_ge(q["r_ranks2"], 3)
                for e in range(EH * h, EH * (h + 1)):
                    for c in range(NT):
                        g = c % 4
                        ins = mm(psJ[NBL * g:NBL * (g + 1), NA * e:NA * (e + 1)], Boh[:, :, NT * e + c], Awt[:, :, NT * e + c],
                                 start=(c < 4), stop=(c >= NT - 4), tile_position=(0, NBL * g), skip_group_check=True)
                ins.then_inc(q["t_list"], 1)

            def spread_lists(h):
                pe.wait_ge(q["r_tok"], h + 1)
                wait(pe, "l_ld", h)
                for j in range(NI):
                    ins = mm(psT[NBL * j:NBL * (j + 1), 1, 0:EH * NI], cst[:, C_STK:C_STK + NBL],
                             tokp[:, EH * h:EH * (h + 1), NI * j:NI * (j + 1)],
                             start=True, stop=True, tile_position=(0, NBL * j), skip_group_check=True)
                ins.then_inc(q["t_idx"], 1)

            routing = [(lambda k=k: search(k)) for k in range(SEARCH)]
            routing += [thresholds, ranks_equal, none, none, ranks_chosen]
            quarters = [(n, m) for n in range(2, NB) for m in range(NM)]
            for n, m in quarters[:2]:
                quarter(n, m)
            for k, (n, m) in enumerate(quarters[2:]):
                if k < len(routing):
                    routing[k]()
                quarter(n, m)
            second(NB - 1, 2)
            second(NB - 1, 3)
            turn_back(NB - 1)
            for h in range(2):
                token_lists(h)
                spread_lists(h)
            pe.wait_ge(q["l_ld"], 2)

            gather_in(0)
            for e in range(E):
                nxt = (lambda e=e: gather_in(e + 1)) if e + 1 < E else none
                block_of(NB + e, [none, none, nxt, none])
            second(NB + E - 1, 2)
            second(NB + E - 1, 3)
            turn_back(NB + E - 1)


_INS = ['x', 'ctx_1024', 'mask_BxS2_bf1', 'L0_xattn_Wq', 'L0_xattn_bq', 'L0_xattn_Wk', 'L0_xattn_bk', 'L0_xattn_Wv',
        'L0_xattn_bv', 'L0_xattn_Wo', 'L0_xattn_bo', 'L0_ffn_gate', 'L0_ffn_W1', 'L0_ffn_b1', 'L0_ffn_W2', 'L0_ffn_b2',
        'L0_ffn_Ws1', 'L0_ffn_bs1', 'L0_ffn_Ws2', 'L0_ffn_bs2']


def kernel(**inputs):
    import concourse.bacc as _bacc
    from concourse.bass_utils import run_bass_kernel_spmd as _run

    nc = _bacc.Bacc("TRN2", target_bir_lowering=False, num_devices=1)
    arrays, args = {}, []
    for name in _INS:
        a = np.ascontiguousarray(inputs[name])
        if a.dtype == np.bool_:
            a = a.view(np.uint8)
        arrays[name] = a
        args.append(nc.dram_tensor(name, a.shape, mybir.dt.from_np(a.dtype), kind="ExternalInput").ap())
    for name, a in zip(("consts", "kbits"), constants()):
        arrays[name] = a
        args.append(nc.dram_tensor(name, a.shape, mybir.dt.from_np(a.dtype), kind="ExternalInput").ap())
    args.append(nc.dram_tensor("out", (B, S, D), F32, kind="ExternalOutput").ap())
    args.append(nc.dram_tensor("gather_table", (T, ROW), F32).ap())
    args.append(nc.dram_tensor("token_lists", (E * CAP,), I32).ap())
    build(nc, *args)
    r = _run(nc, [arrays], core_ids=[0])
    return r.results[0]["out"]
```

```python
from contextlib import ExitStack

import numpy as np

import concourse.bass as bass
from concourse import mybir

F32 = mybir.dt.float32
BF16 = mybir.dt.bfloat16
F16 = mybir.dt.float16
I32 = mybir.dt.int32
U32 = mybir.dt.uint32
U8 = mybir.dt.uint8
ALU = mybir.AluOpType
ACT = mybir.ActivationFunctionType
AX = mybir.AxisListType

P = 128
B, S, D = 64, 64, 128
H, DH = 16, 8
T = B * S
NT = T // P
UT = 2
NU = NT // UT
E = 8
F = 512
NM = F // P
CAP = T // E
NI = CAP // P
FB = 512
NB = T // FB
EPS = 1e-5
MASKED = 1e30
SCALE = float(DH) ** -0.5
BITS = 30
SEARCH = BITS // 2
NA, NBL = 16, 32
PARTS = ((0, 2), (2, E))
GAHEAD = 5
NG = 7
ROW = D + E

C_ID, C_J, C_PM, C_STK, C_SAME, C_TRI = 0, 128, 132, 134, 166, 294
C_SEG, C_TOK, C_IND = 422, 678, 934
C_END = C_IND + 128
R_B1, R_BS1, R_B2, R_BS2, R_BQ, R_BK, R_BV, R_BO = 0, 32, 36, 44, 45, 46, 47, 48
NR = 49


def constants():
    r = np.arange(P)
    c = np.zeros((P, C_END), np.float32)
    c[:, C_ID:C_ID + P] = np.eye(P)
    c[:, C_J:C_J + 4] = (r[:, None] // DH) % 4 == np.arange(4)
    c[:, C_PM:C_PM + 2] = (r[:, None] // (2 * DH)) % 2 == np.arange(2)
    c[:, C_STK:C_STK + NBL] = r[:, None] % NBL == np.arange(NBL)
    c[:, C_SAME:C_SAME + P] = r[:, None] % E == r % E
    c[:, C_TRI:C_TRI + P] = (r[:, None] < r) - 1.0
    c[:, C_SEG:C_SEG + E * NT] = (np.arange(E * NT) % NT) != 0
    c[:, C_TOK:C_TOK + E * NT] = r[:, None] + P * (np.arange(E * NT) % NT) - T // 2
    c[0:2, C_IND:C_IND + P] = np.arange(2)[:, None] == r // 64
    k = (np.arange(4)[None, :] << (BITS - 2 - 2 * np.arange(SEARCH))[:, None]).astype(np.int32)
    return c, np.broadcast_to(k.reshape(1, -1), (P, 4 * SEARCH)).copy()


def build(nc, x, ctx_in, mask, W1, W2, Ws1, Ws2, weights, biases, consts, kbits, out, table):
    es = ExitStack()
    with es:
        def sb(name, shape, dt=F32):
            return es.enter_context(nc.sbuf_tensor(name, shape, dt))

        def sem(name):
            return es.enter_context(nc.semaphore(name))

        cst = sb("cst", [P, C_END])
        kb = sb("kb", [P, SEARCH, 4], I32)
        ident = cst[:, C_ID:C_ID + P]
        bias_rows = sb("bias_rows", [NR, P])
        bias_c = sb("bias_c", [P, NR])
        bo2 = sb("bo2", [P, 1])
        w_all = sb("w_all", [P, 4 * D + E])
        wqkv = w_all[:, 0:3 * D].rearrange("p (k d) -> p k d", k=3)
        wo = w_all[:, 3 * D:4 * D]
        gate_w = w_all[:, 4 * D:]
        wom = sb("wom", [P, 2, D])
        mask8 = sb("mask8", [2, NT, S], U8)
        maskr = sb("maskr", [2, NT, S], BF16)
        ind = sb("ind", [2, P], BF16)
        same = sb("same", [P, P], BF16)
        tri = sb("tri", [P, P], BF16)
        ones = sb("ones", [P, P], BF16)
        tokh = sb("tokh", [P, E * NT], F16)
        X = sb("X", [P, NT, D])
        cin = sb("cin", [P, 2, UT, D])
        st1 = sb("st1", [P, 2, UT, 6])
        mv1 = sb("mv1", [P, 2, UT, 2])
        rs1 = sb("rs1", [P, 2, UT])
        st2 = sb("st2", [P, 2, UT, 6])
        mv2 = sb("mv2", [P, 2, UT, 2])
        rs2 = sb("rs2", [P, 2, UT])
        mhalf = sb("mhalf", [P, UT])
        xh1 = sb("xh1", [P, 2, UT, D])
        xcT = sb("xcT", [P, 2, 2 * UT, P])
        QT = sb("QT", [P, 2, UT * P])
        KT = sb("KT", [P, 2, UT * P])
        Kbd = sb("Kbd", [P, 2, 4, UT * P])
        Vz = sb("Vz", [P, 2, 4, D])
        held = sb("held", [P, 2])
        held_a = sb("held_a", [P, 1])
        mx = sb("mx", [P, 2, H])
        Pn = sb("Pn", [P, 2, 2, H * S])
        PTs = sb("PTs", [P, 2, 8, P])
        sums = sb("sums", [P, 2, H])
        rsum = sb("rsum", [P, 2, H])
        OLn = sb("OLn", [P, 2, 4, P])
        yTs = sb("yTs", [P, 2, UT * P])
        xh2 = sb("xh2", [P, 2, UT, D])
        x2Ts = sb("x2Ts", [P, 2, UT * P])
        X2T = sb("X2T", [P, T])
        lg = sb("lg", [P, NT, E])
        mxl = sb("mxl", [P, NT])
        pe_ = sb("pe_", [P, NT, E])
        sml = sb("sml", [P, NT])
        rsl = sb("rsl", [P, NT])
        pr8 = sb("pr8", [P, NT, E])
        prT = sb("prT", [P, 2 * P])
        cand = sb("cand", [P, 4], I32)
        cur = sb("cur", [P, 1])
        junk = sb("junk", [P, 3, 2 * P], BF16)
        cnt = sb("cnt", [P, 4], BF16)
        kept = sb("kept", [P, 4])
        thr_b = sb("thr_b", [P, P])
        thr = sb("thr", [P, E])
        gtm = sb("gtm", [P, E, NT], BF16)
        eqm = sb("eqm", [P, E, NT], BF16)
        selm = sb("selm", [P, E, NT], BF16)
        scn = sb("scn", [P, E, NT])
        rk = sb("rk", [P, E, NT])
        rk2 = sb("rk2", [P, E, NT])
        gcn = sb("gcn", [P, E])
        need = sb("need", [P, E])
        posi = sb("posi", [P, E * NT], I32)
        pa = sb("pa", [P, E * NT], I32)
        pb = sb("pb", [P, E * NT], I32)
        pab = sb("pab", [P, E * NT], F16)
        pbb = sb("pbb", [P, E * NT], F16)
        Awt = sb("Awt", [P, NA, E * NT], F16)
        Boh = sb("Boh", [P, NBL, E * NT], F16)
        tokp = sb("tokp", [P, E, NA])
        idx = sb("idx", [P, E, NI], U32)
        ws1 = sb("ws1", [P, F])
        ws2 = sb("ws2", [P, NM, D])
        w1 = sb("w1", [P, E, F])
        w2 = sb("w2", [P, E, NM, D])
        hT = sb("hT", [P, NM, FB])
        yT = sb("yT", [P, FB])
        yo = sb("yo", [P, 2, NI, D])
        gx = Pn[:].rearrange("p a b k -> p (a b k)")[:, 0:NG * NI * ROW].rearrange("p (g i w) -> p g i w", g=NG, i=NI)
        xeT = sb("xeT", [P, 2, CAP])

        psS = es.enter_context(nc.psum_tensor("psS", [P, 4, 512], F32))
        psT = es.enter_context(nc.psum_tensor("psT", [P, 2, 512], F32))
        psO = es.enter_context(nc.psum_tensor("psO", [P, 512], F32))
        psJ = es.enter_context(nc.psum_tensor("psJ", [P, 512], F32))

        names = """c_ld ct_ld act_tab br_ld w_ld m_ld kb_ld wf_ld x_ld0 x_ld1 x_ld2 x_ld3 ctx_ld0 ctx_ld1 tab_st0 tab_st1
            pe_bias bias_ok bo2_mm bo2_ok cdve cpool mrow
            v_st1 v_ag1 v_ve1 pl_rs1 v_xh1 v_max v_sub v_sum v_rec a_o pl_pn v_x1 v_st2 v_ag2 v_ve2 pl_rs2 v_xh2
            v_gate v_v a_xt a_q a_k a_v a_exp a_pt a_y pl_x2 a_x2t pl_kbd
            t_xt t_qk t_v t_S0 t_S t_T t_O t_y t_yt t_x2t t_g
            r_step r_p r_prT r_tT r_prs p_st s_cnt s_tot s_upd s_fin t_thr r_m r_ranks r_m2 r_need r_ranks2 r_pos
            w_tok b_oh t_list r_tok t_idx l_ld
            t_h a_h t_yy a_yy t_yo a_ys pl_ys v_yo o_st0 o_st1 g_ld0 g_ld1 g_ld2 g_ld3 g_ld4 g_ld5 g_ld6 t_xe a_xe we_ld sc_st0 sc_st1""".split()
        q = {n: sem(n) for n in names}
        x_ld = [q[f"x_ld{k}"] for k in range(4)]
        ctx_ld = [q["ctx_ld0"], q["ctx_ld1"]]
        tab_st = [q["tab_st0"], q["tab_st1"]]
        g_ld = [q[f"g_ld{k}"] for k in range(NG)]
        o_st = [q["o_st0"], q["o_st1"]]
        sc_st = [q["sc_st0"], q["sc_st1"]]

        x_v = x.rearrange("a s d -> (a s) d").rearrange("(c p) d -> p c d", p=P)
        ctx_v = ctx_in.rearrange("a s d -> (a s) d").rearrange("(c p) d -> p c d", p=P)
        out_rows = out.rearrange("a s d -> (a s) d")
        out_v = out_rows.rearrange("(c p) d -> p c d", p=P)
        tab_v = table.rearrange("(c p) w -> p c w", p=P)

        FIRST, LAST = -2, NU + 3
        LOOP0, NLOOP = 4, (NU - 3 - 4) // 2

        class Step:

            def __init__(self, i, u0, looped):
                self.i, self.u0, self.looped = i, u0, looped

            def u(self, k):
                return 2 * self.i + (self.u0 + k) if self.looped else self.u0 + k

            def half(self, k):
                return self.i + (self.u0 + k) // 2 if self.looped else (self.u0 + k) // 2

            def par(self, k):
                return (self.u0 + k) % 2

            def on(self, k):
                return self.looped or 0 <= self.u0 + k < NU

        def pipeline(eng, body):
            for u in range(FIRST, LOOP0):
                body(Step(0, u, False))
            with eng.Fori(0, NLOOP) as i:
                body(Step(i, LOOP0, True))
                body(Step(i, LOOP0 + 1, True))
            for u in range(LOOP0 + 2 * NLOOP, LAST):
                body(Step(0, u, False))

        FILL = {(NU, "g"): [(0, 0)], (NU + 1, "y"): [(0, 1)], (NU + 1, "yt"): [(0, 2)], (NU + 1, "x2t"): [(0, 3)],
                (NU + 2, "g"): [(1, 0), (1, 1)]}

        def fill(s, stage, quarter):
            if not s.looped:
                for n, m in FILL.get((s.u0, stage), []):
                    quarter(n, m)

        def wait(eng, s, value):
            if not isinstance(value, int) or value > 0:
                eng.wait_ge(q[s] if isinstance(s, str) else s, value)

        def columns(h):
            return slice(NT * PARTS[h][0], NT * PARTS[h][1])

        block = es.enter_context(nc.Block())

        @block.sync
        def _(sp):
            sp.dma_start(X[:, 0:UT, :], x_v[:, 0:UT, :]).then_inc(x_ld[0], 16)
            sp.dma_start(cst[:, 0:C_STK], consts[:, 0:C_STK]).then_inc(q["c_ld"], 16)
            sp.dma_start(cin[:, 0], ctx_v[:, 0:UT, :]).then_inc(ctx_ld[0], 16)
            sp.dma_start(cst[:, C_STK:], consts[:, C_STK:]).then_inc(q["ct_ld"], 16)
            sp.dma_start(cin[:, 1], ctx_v[:, UT:2 * UT, :]).then_inc(ctx_ld[1], 16)
            for k, (c0, c1) in enumerate(((UT, NT // 4), (NT // 4, NT // 2), (NT // 2, NT)), 1):
                sp.dma_start(X[:, c0:c1, :], x_v[:, c0:c1, :]).then_inc(x_ld[k], 16)

            def body(s):
                if s.on(3) and (s.looped or s.u0 + 3 >= 2):
                    wait(sp, "t_xt", s.u(2))
                    sp.dma_start(cin[:, s.par(3)], ctx_v[:, bass.ds(UT * s.u(3), UT), :]).then_inc(
                        ctx_ld[s.par(3)], 16)
                if s.on(-2):
                    wait(sp, "v_xh2", s.u(-1))
                    sp.dma_start(tab_v[:, bass.ds(UT * s.u(-2), UT), 0:D], xh2[:, s.par(-2)]).then_inc(
                        tab_st[s.par(-2)], 16)

            pipeline(sp, body)
            sp.dma_start(w1[:], W1.rearrange("e p f -> p e f")).then_inc(q["we_ld"], 16)
            for e in range(E):
                sp.dma_start(w2[:, e], W2[e].rearrange("(m p) d -> p m d", p=P)).then_inc(q["we_ld"], 16)
            sp.wait_ge(q["r_p"], 1)
            sp.dma_start(tab_v[:, :, D:ROW], pr8[:]).then_inc(q["p_st"], 16)
            for b in range(NB):
                sp.wait_ge(q["pl_ys"], b + 1)
                sp.dma_start(out_v[:, NI * b:NI * b + NI, :], yo[:, b % 2]).then_inc(o_st[b % 2], 16)
            for p in range(2):
                sp.wait_ge(o_st[p], 16 * (NB // 2))

        def y_evac(act, n):
            act.wait_ge(q["t_yy"], NM * (n + 1))
            wait(act, "t_yo", n)
            b = R_BS2 if n < NB else R_B2 + n - NB
            nc.scalar.activation(yT[:], psO[:], ACT.Identity, bias=bias_c[:, b:b + 1]).then_inc(q["a_yy"], 1)

        @block.scalar
        def _(act):
            act.dma_start(bias_rows[:], biases).then_inc(q["br_ld"], 16)
            act.dma_start(w_all[:], weights).then_inc(q["w_ld"], 16)
            act.dma_start(mask8[:], mask.rearrange("(i b) k -> b i k", b=2)).then_inc(q["m_ld"], 16)
            act.wait_ge(q["cpool"], 1)
            nc.scalar.activation(held_a[:], mhalf[:, 0:1], ACT.Exp).then_inc(q["act_tab"], 1)
            act.wait_ge(q["pe_bias"], 1)
            nc.scalar.copy(bias_c[:], psJ[:, 0:NR]).then_inc(q["bias_ok"], 1)
            act.wait_ge(q["bo2_mm"], 1)
            act.wait_ge(q["bias_ok"], 1)
            nc.scalar.activation(bo2[:], psJ[:, 0:1], ACT.Identity, bias=bias_c[:, R_BO:R_BO + 1]).then_inc(q["bo2_ok"], 1)
            act.dma_start(kb[:], kbits.rearrange("p (s k) -> p s k", k=4)).then_inc(q["kb_ld"], 16)
            act.dma_start(ws1[:], Ws1).then_inc(q["wf_ld"], 16)
            act.dma_start(ws2[:], Ws2.rearrange("(m p) d -> p m d", p=P)).then_inc(q["wf_ld"], 16)

            def hidden_out(n, m):
                if m == 2 and n > 0 and n != NB:
                    y_evac(act, n - 1)
                act.wait_ge(q["t_h"], NM * n + m + 1)
                wait(act, "t_yy", NM * (n - 1) + m + 1)
                if (n, m) == (1, 1):
                    act.wait_ge(q["r_step"], 2)
                    nc.scalar.activation(pe_[:], pe_[:], ACT.Exp).then_inc(q["r_prs"], 1)
                b = R_BS1 + m if n < NB else R_B1 + NM * (n - NB) + m
                nc.scalar.activation(hT[:, m], psS[:, m], ACT.Gelu_apprx_tanh, bias=bias_c[:, b:b + 1]).then_inc(q["a_h"], 1)
                if m == 2 and 0 < n < NB:
                    shared_out(n - 1)

            def gathered(e):
                act.wait_ge(q["t_xe"], e + 1)
                if e >= 2:
                    act.wait_ge(q["t_h"], NM * (NB + e - 1))
                nc.scalar.copy(xeT[:, e % 2], psT[:, 1]).then_inc(q["a_xe"], 1)

            def shared_out(b):
                act.wait_ge(q["t_yo"], b + 1)
                if b >= 2:
                    act.wait_ge(o_st[b % 2], 16 * (b // 2))
                nc.scalar.copy(yo[:, b % 2], psT[:, 0].rearrange("p (a d) -> p a d", a=NI)).then_inc(q["a_ys"], 1)

            def pt_evac(s, k, pr, hf):
                wait(act, "t_T", 4 * s.u(k) + 2 * pr + hf + 1)
                wait(act, "t_O", 2 * s.u(k) + pr - 1)
                nc.scalar.copy(PTs[:, pr, 4 * hf:4 * hf + 4, :], psT[:, hf].rearrange("p (a t) -> p a t", a=4)).then_inc(q["a_pt"], 1)

            def exps(s, pr):
                wait(act, "v_sub", 2 * s.u(0) + pr + 1)
                nc.scalar.activation(Pn[:, s.par(0), pr], Pn[:, s.par(0), pr], ACT.Exp, scale=SCALE).then_inc(q["a_exp"], 1)

            def body(s):
                if s.on(-2):
                    wait(act, "t_y", s.u(-1))
                    wait(act, "t_yt", s.u(-3))
                    nc.scalar.activation(yTs[:, s.par(-2)], psJ[:, 0:UT * P], ACT.Identity, bias=bo2[:, 0:1]).then_inc(q["a_y"], 1)
                fill(s, "y", hidden_out)
                fill(s, "yt", hidden_out)
                if s.on(1):
                    wait(act, "t_xt", s.u(2))
                    wait(act, "t_v", s.u(0))
                    nc.scalar.copy(xcT[:, s.par(1)], psJ.rearrange("p (a t) -> p a t", a=4)).then_inc(q["a_xt"], 1)
                if s.on(0):
                    exps(s, 0)
                if s.on(-1):
                    pt_evac(s, -1, 0, 0)
                    pt_evac(s, -1, 0, 1)
                if s.on(1):
                    wait(act, "t_qk", s.u(2))
                    wait(act, "t_S", 2 * s.u(0))
                    wait(act, "pl_kbd", s.u(0))
                    nc.scalar.activation(KT[:, s.par(1)], psJ[:, UT * P:2 * UT * P], ACT.Identity, bias=bias_c[:, R_BK:R_BK + 1]).then_inc(q["a_k"], 1)
                    nc.scalar.activation(QT[:, s.par(1)], psJ[:, 0:UT * P], ACT.Identity, bias=bias_c[:, R_BQ:R_BQ + 1]).then_inc(q["a_q"], 1)
                if s.on(-3):
                    wait(act, "t_x2t", s.u(-2))
                    wait(act, "t_g", s.u(-4))
                    wait(act, "pl_x2", s.u(-4))
                    nc.scalar.copy(x2Ts[:, s.par(-3)], psJ[:, 0:UT * P]).then_inc(q["a_x2t"], 1)
                fill(s, "x2t", hidden_out)
                if s.on(-1):
                    pt_evac(s, -1, 1, 0)
                    pt_evac(s, -1, 1, 1)
                if s.on(0):
                    exps(s, 1)
                if s.on(1):
                    wait(act, "t_v", s.u(2))
                    wait(act, "t_O", 2 * s.u(0))
                    v = psJ[0:64, :].rearrange("p (b g h d) -> p b g h d", b=4, h=2, d=DH)
                    o = Vz[0:64, s.par(1)].rearrange("p b (g h d) -> p b g h d", h=2, d=DH)
                    nc.scalar.copy(o[:, :, :, 0, :], v[:, :, :, 0, :]).then_inc(q["a_v"], 1)
                if s.on(-1):
                    wait(act, "t_O", 2 * s.u(0))
                    wait(act, "t_y", s.u(-2))
                    nc.scalar.copy(OLn[:, s.par(-1)], psO.rearrange("p (b t) -> p b t", b=4)).then_inc(q["a_o"], 1)
                fill(s, "g", hidden_out)

            act.wait_ge(q["cpool"], 2)
            pipeline(act, body)

            hidden_out(1, 2)
            hidden_out(1, 3)
            for n in range(2, NB + E):
                e = n - NB
                if e == 0:
                    y_evac(act, n - 1)
                    gathered(0)
                    shared_out(n - 1)
                for m in range(NM):
                    hidden_out(n, m)
                    if m == 2 and 0 <= e < E - 1:
                        gathered(e + 1)
            y_evac(act, NB + E - 1)

        @block.gpsimd
        def _(pool):
            nc.gpsimd.memset(mhalf[:], -0.5).then_inc(q["cpool"], 1)
            nc.gpsimd.memset(Vz[:], 0.0).then_inc(q["cpool"], 1)
            pool.wait_ge(q["c_ld"], 16)

            def normalise(s, pr):
                wait(pool, "v_rec", 2 * s.u(0) + pr + 1)
                pn = Pn[:, s.par(0), pr].rearrange("p (h k) -> p h k", k=S)
                nc.gpsimd.tensor_tensor(pn, pn, rsum[:, pr].unsqueeze(2).to_broadcast([P, H, S]), ALU.mult).then_inc(q["pl_pn"], 1)

            def body(s):
                if s.on(1):
                    wait(pool, "a_k", s.u(2))
                    wait(pool, "t_S", 2 * s.u(0))
                    nc.gpsimd.tensor_tensor(
                        Kbd[:, s.par(1)],
                        KT[:, s.par(1)].unsqueeze(1).to_broadcast([P, 4, UT * P]),
                        cst[:, C_J:C_J + 4].unsqueeze(2).to_broadcast([P, 4, UT * P]), ALU.mult).then_inc(q["pl_kbd"], 1)
                if s.on(-2):
                    wait(pool, "v_ve2", s.u(-1))
                    wait(pool, "v_xh2", s.u(-3))
                    nc.gpsimd.tensor_tensor(rs2[:, s.par(-2)], mv2[:, s.par(-2), :, 1], mhalf[:], ALU.pow).then_inc(q["pl_rs2"], 1)
                if s.on(2):
                    wait(pool, "v_ve1", s.u(3))
                    wait(pool, "v_xh1", s.u(1))
                    nc.gpsimd.tensor_tensor(rs1[:, s.par(2)], mv1[:, s.par(2), :, 1], mhalf[:], ALU.pow).then_inc(q["pl_rs1"], 1)
                if s.on(-3):
                    wait(pool, "a_x2t", s.u(-2))
                    nc.gpsimd.tensor_copy(X2T[:, bass.ds(UT * P * s.u(-3), UT * P)], x2Ts[:, s.par(-3)]).then_inc(q["pl_x2"], 1)
                if s.on(0):
                    normalise(s, 0)
                if s.on(0):
                    normalise(s, 1)

            pool.wait_ge(q["cpool"], 2)
            pipeline(pool, body)

            def residual(b):
                pool.wait_ge(q["a_ys"], b + 1)
                nc.gpsimd.tensor_tensor(yo[:, b % 2], yo[:, b % 2], X[:, NI * b:NI * b + NI, :], ALU.add).then_inc(q["pl_ys"], 1)

            def gather(e):
                if e >= NG:
                    pool.wait_ge(q["v_yo"], e - NG + 1)
                pool.wait_ge(q["l_ld"], 1 if e < PARTS[0][1] else 2)
                for i in range(NI):
                    pool.indirect_dma_start(
                        out=gx[:, e % NG, i, :], out_offset=None, in_=table[:, :],
                        in_offset=bass.IndirectOffsetOnAxis(ap=idx[:, e, i:i + 1], axis=0)).then_inc(g_ld[e % NG], 16)

            for b in range(NB - 2):
                residual(b)
            for p in range(2):
                pool.wait_ge(tab_st[p], 16 * (NU // 2))
            pool.wait_ge(q["p_st"], 16)
            gather(0)
            residual(NB - 2)
            residual(NB - 1)
            for e in range(1, GAHEAD):
                gather(e)
            for p in range(2):
                pool.wait_ge(o_st[p], 16 * (NB // 2))
            for e in range(E):
                pool.wait_ge(q["v_yo"], e + 1)
                if e:
                    pool.wait_ge(sc_st[(e - 1) % 2], 16 * NI * ((e - 1) // 2 + 1))
                for i in range(NI):
                    pool.indirect_dma_start(
                        out=out_rows, out_offset=bass.IndirectOffsetOnAxis(ap=idx[:, e, i:i + 1], axis=0),
                        in_=yo[:, e % 2, i, :], in_offset=None, compute_op=ALU.add).then_inc(sc_st[e % 2], 16)
                if e + GAHEAD < E:
                    gather(e + GAHEAD)
            for p in range(2):
                pool.wait_ge(sc_st[p], 16 * NI * (E // 2))

        @block.vector
        def _(dve):
            def tables():
                dve.wait_ge(q["ct_ld"], 16)
                nc.vector.tensor_copy(ind[:], cst[0:2, C_IND:C_IND + P]).then_inc(q["cdve"], 1)
                dve.wait_ge(q["m_ld"], 16)
                nc.vector.tensor_scalar(maskr[:], mask8[:], 1.0, MASKED, ALU.subtract, ALU.mult).then_inc(q["mrow"], 1)
                dve.wait_ge(q["c_ld"], 16)
                dve.wait_ge(q["w_ld"], 16)
                for k in range(2):
                    nc.vector.tensor_scalar(wom[:, k], wo, cst[:, C_PM + k:C_PM + k + 1], None, ALU.mult).then_inc(q["cdve"], 1)
                nc.vector.tensor_copy(same[:], cst[:, C_SAME:C_SAME + P]).then_inc(q["cdve"], 1)
                nc.vector.tensor_copy(tri[:], cst[:, C_TRI:C_TRI + P]).then_inc(q["cdve"], 1)
                nc.vector.memset(ones[:], 1.0).then_inc(q["cdve"], 1)
                nc.vector.tensor_copy(tokh[:], cst[:, C_TOK:C_TOK + E * NT]).then_inc(q["cdve"], 1)

            def stats(v, par, c0, st, mv, n_st, n_ag, n_ve):
                nc.vector.memset(held[:, 0:1], 0.0)
                for t in range(UT):
                    nc.vector.bn_stats(st[:, par, t], X[:, bass.ds(c0 + t, 1), :].rearrange("p a d -> p (a d)")).then_inc(q[n_st], 1)
                wait(dve, n_st, UT * (v + 1))
                nc.vector.memset(held[:, 1:2], 0.0)
                for t in range(UT):
                    nc.vector.bn_aggr(mv[:, par, t], st[:, par, t]).then_inc(q[n_ag], 1)
                wait(dve, n_ag, UT * (v + 1))
                nc.vector.tensor_scalar(mv[:, par, :, 1], mv[:, par, :, 1], EPS, None, ALU.add).then_inc(q[n_ve], 1)

            def normed(dst, par, c0, mv, rs, name):
                for t in range(UT):
                    ins = nc.vector.tensor_scalar(dst[:, par, t], X[:, bass.ds(c0 + t, 1), :].rearrange("p a d -> p (a d)"),
                                                  mv[:, par, t, 0:1], rs[:, par, t:t + 1], ALU.subtract, ALU.mult)
                ins.then_inc(q[name], 1)

            def centre(s, pr):
                wait(dve, "t_S", 2 * s.u(0) + pr + 1)
                z = psS[:, 2 * pr:2 * pr + 2, :].rearrange("p a (h k) -> p (a h) k", k=S)
                nc.vector.tensor_reduce(mx[:, pr], z, AX.X, ALU.max).then_inc(q["v_max"], 1)
                wait(dve, "v_max", 2 * s.u(0) + pr + 1)
                wait(dve, "t_T", 4 * s.u(-2) + 2 * pr + 2)
                nc.vector.tensor_tensor(Pn[:, s.par(0), pr].rearrange("p (h k) -> p h k", k=S), z,
                                        mx[:, pr].unsqueeze(2).to_broadcast([P, H, S]), ALU.subtract).then_inc(q["v_sub"], 1)

            def row_sums(s, pr):
                n = 2 * s.u(0) + pr + 1
                wait(dve, "a_exp", n)
                nc.vector.tensor_reduce(sums[:, pr], Pn[:, s.par(0), pr].rearrange("p (h k) -> p h k", k=S), AX.X, ALU.add).then_inc(q["v_sum"], 1)
                wait(dve, "v_sum", n)
                wait(dve, "pl_pn", n - 2)
                nc.vector.reciprocal(rsum[:, pr], sums[:, pr]).then_inc(q["v_rec"], 1)

            def body(s):
                if not s.looped and s.u0 == FIRST:
                    dve.wait_ge(x_ld[0], 16)
                if not s.looped and s.u0 == FIRST + 1:
                    tables()
                    for k in range(1, 4):
                        dve.wait_ge(x_ld[k], 16)
                if s.on(-2):
                    wait(dve, "t_yt", s.u(-1))
                    xs = X[:, bass.ds(UT * s.u(-2), UT), :].rearrange("p a d -> p (a d)")
                    nc.vector.tensor_tensor(xs, xs, psJ[:, 0:UT * P], ALU.add).then_inc(q["v_x1"], 1)
                if s.on(0):
                    centre(s, 0)
                    centre(s, 1)
                if s.on(-2):
                    wait(dve, "v_x1", s.u(-1))
                    stats(s.u(-2), s.par(-2), UT * s.u(-2), st2, mv2, "v_st2", "v_ag2", "v_ve2")
                if s.on(2):
                    stats(s.u(2), s.par(2), UT * s.u(2), st1, mv1, "v_st1", "v_ag1", "v_ve1")
                if s.on(0):
                    row_sums(s, 0)
                if s.on(1):
                    wait(dve, "t_v", s.u(2))
                    wait(dve, "t_O", 2 * s.u(0))
                    v = psJ[64:128, :].rearrange("p (b g h d) -> p b g h d", b=4, h=2, d=DH)
                    o = Vz[64:128, s.par(1)].rearrange("p b (g h d) -> p b g h d", h=2, d=DH)
                    nc.vector.tensor_copy(o[:, :, :, 1, :], v[:, :, :, 1, :]).then_inc(q["v_v"], 1)
                if s.on(0):
                    row_sums(s, 1)
                def gate_out():
                    wait(dve, "t_g", s.u(-2))
                    nc.vector.tensor_copy(lg[:, bass.ds(UT * s.u(-3), UT), :].rearrange("p a e -> p (a e)"), psT[:, 0, 0:UT * E]).then_inc(q["v_gate"], 1)

                def normed_2():
                    wait(dve, "pl_rs2", s.u(-1))
                    wait(dve, "t_x2t", s.u(-3))
                    wait(dve, tab_st[s.par(-2)], 16 * s.half(-2))
                    normed(xh2, s.par(-2), UT * s.u(-2), mv2, rs2, "v_xh2")

                if s.on(-2) and not s.on(0):
                    normed_2()
                if s.on(-3):
                    gate_out()
                if s.on(-2) and s.on(0):
                    normed_2()
                if s.on(2):
                    wait(dve, "pl_rs1", s.u(3))
                    wait(dve, "t_xt", s.u(1))
                    normed(xh1, s.par(2), UT * s.u(2), mv1, rs1, "v_xh1")

            dve.wait_ge(q["cpool"], 2)
            pipeline(dve, body)

            dve.wait_ge(q["v_gate"], NU)
            nc.vector.tensor_reduce(mxl[:], lg[:], AX.X, ALU.max).then_inc(q["r_step"], 1)
            dve.wait_ge(q["r_step"], 1)
            nc.vector.tensor_tensor(pe_[:], lg[:], mxl[:].unsqueeze(2).to_broadcast([P, NT, E]), ALU.subtract).then_inc(q["r_step"], 1)
            dve.wait_ge(q["r_prs"], 1)
            nc.vector.tensor_reduce(sml[:], pe_[:], AX.X, ALU.add).then_inc(q["r_step"], 1)
            dve.wait_ge(q["r_step"], 3)
            nc.vector.reciprocal(rsl[:], sml[:]).then_inc(q["r_step"], 1)
            dve.wait_ge(q["r_step"], 4)
            nc.vector.tensor_tensor(pr8[:], pe_[:], rsl[:].unsqueeze(2).to_broadcast([P, NT, E]), ALU.mult).then_inc(q["r_p"], 1)
            dve.wait_ge(q["r_tT"], 1)
            nc.vector.tensor_copy(prT[:], psT[:, 1, 0:2 * P]).then_inc(q["r_prT"], 1)
            nc.vector.memset(cnt[:, 0:1], float(2 * P)).then_inc(q["s_upd"], 1)
            dve.wait_ge(q["kb_ld"], 16)
            nc.vector.tensor_copy(cand[:], kb[:, 0]).then_inc(q["s_upd"], 1)
            dve.wait_ge(q["r_prT"], 1)

            for k in range(SEARCH):
                dve.wait_ge(q["s_upd"], 2 + 3 * k)
                if k:
                    dve.wait_ge(q["s_tot"], k)
                for j in range(1, 4):
                    with nc.allow_low_precision(reason="counts up to 256 are exact"):
                        ins = nc.vector.tensor_scalar(junk[:, j - 1], prT[:], cand[:, j:j + 1].bitcast(F32), 0.0, ALU.is_ge, ALU.add,
                                                      accum_out=cnt[:, j:j + 1])
                    ins.then_inc(q["s_cnt"], 1)
                dve.wait_ge(q["s_tot"], k + 1)
                nc.vector.scalar_tensor_tensor(out=kept[:], in0=psT[:, 1, 0:4], scalar=float(CAP), in1=cand[:].bitcast(F32),
                                               op0=ALU.is_ge, op1=ALU.mult).then_inc(q["s_upd"], 1)
                dve.wait_ge(q["s_upd"], 2 + 3 * k + 1)
                nc.vector.tensor_reduce(cur[:], kept[:], AX.X, ALU.max).then_inc(q["s_upd"], 1)
                dve.wait_ge(q["s_upd"], 2 + 3 * k + 2)
                if k + 1 < SEARCH:
                    nc.vector.tensor_tensor(cand[:], kb[:, k + 1], cur[:].bitcast(I32).to_broadcast([P, 4]), ALU.bitwise_or).then_inc(q["s_upd"], 1)
            nc.vector.tensor_copy(thr_b[:], cur[:].to_broadcast([P, P])).then_inc(q["s_fin"], 1)
            dve.wait_ge(q["t_thr"], 1)
            nc.vector.tensor_copy(thr[:], psT[:, 1, 0:E]).then_inc(q["s_fin"], 1)
            dve.wait_ge(q["s_fin"], 2)
            tb = thr[:].unsqueeze(1).to_broadcast([P, NT, E])
            nc.vector.tensor_tensor(gtm[:].rearrange("p e c -> p c e"), pr8[:], tb, ALU.is_gt).then_inc(q["r_m"], 1)
            nc.vector.tensor_tensor(eqm[:].rearrange("p e c -> p c e"), pr8[:], tb, ALU.is_equal).then_inc(q["r_m"], 1)

            def ranks(name):
                less, tot = psJ[:, 0:E * NT], psJ[:, E * NT:2 * E * NT]
                nc.vector.tensor_tensor_scan(scn[:].rearrange("p e c -> p (e c)"), cst[:, C_SEG:C_SEG + E * NT], tot, 0.0,
                                             ALU.mult, ALU.add).then_inc(q[name], 1)
                dve.wait_ge(q[name], 1)
                nc.vector.tensor_tensor(rk2[:].rearrange("p e c -> p (e c)"), scn[:].rearrange("p e c -> p (e c)"), less, ALU.add).then_inc(q[name], 1)

            dve.wait_ge(q["r_ranks"], 1)
            nc.vector.tensor_reduce(gcn[:], psT[:, 1, 0:E * NT].rearrange("p (e c) -> p e c", e=E), AX.X, ALU.add).then_inc(q["r_need"], 1)
            ranks("r_m2")
            dve.wait_ge(q["r_need"], 1)
            nc.vector.tensor_scalar(need[:], gcn[:], -1.0, float(CAP), ALU.mult, ALU.add).then_inc(q["r_need"], 1)
            dve.wait_ge(q["r_need"], 2)
            dve.wait_ge(q["r_m2"], 2)
            nc.vector.tensor_tensor(rk[:], rk2[:], need[:].unsqueeze(2).to_broadcast([P, E, NT]), ALU.is_lt).then_inc(q["r_m2"], 1)
            dve.wait_ge(q["r_m2"], 3)
            nc.vector.tensor_tensor(scn[:], rk[:], eqm[:], ALU.mult).then_inc(q["r_m2"], 1)
            dve.wait_ge(q["r_m2"], 4)
            nc.vector.tensor_tensor(selm[:], scn[:], gtm[:], ALU.add).then_inc(q["r_m"], 1)
            dve.wait_ge(q["r_ranks"], 2)
            dve.wait_ge(q["r_m"], 3)
            ranks("r_ranks2")
            dve.wait_ge(q["r_ranks2"], 2)
            nc.vector.scalar_tensor_tensor(out=posi[:], in0=selm[:].rearrange("p e c -> p (e c)"), scalar=2.0 * CAP,
                                           in1=rk2[:].rearrange("p e c -> p (e c)"), op0=ALU.mult, op1=ALU.add).then_inc(q["r_ranks2"], 1)
            dve.wait_ge(q["r_ranks2"], 3)
            nc.vector.tensor_scalar(pb[:], posi[:], NBL - 1, None, ALU.bitwise_and).then_inc(q["r_ranks2"], 1)
            nc.vector.tensor_scalar(pa[:], posi[:], NBL.bit_length() - 1, None, ALU.logical_shift_right).then_inc(q["r_ranks2"], 1)
            dve.wait_ge(q["r_ranks2"], 4)
            nc.vector.tensor_copy(pbb[:], pb[:]).then_inc(q["r_pos"], 1)
            dve.wait_ge(q["r_ranks2"], 5)
            nc.vector.tensor_copy(pab[:], pa[:]).then_inc(q["r_pos"], 1)
            dve.wait_ge(q["r_pos"], 2)

            def one_hot_low(h, i0=0, i1=NBL):
                for i in range(i0, i1):
                    nc.vector.tensor_scalar(Boh[:, i, columns(h)], pbb[:, columns(h)], float(i), None, ALU.is_equal).then_inc(q["b_oh"], 1)

            def one_hot_high(h, i0, i1):
                for i in range(i0, i1):
                    nc.vector.scalar_tensor_tensor(out=Awt[:, i, columns(h)], in0=pab[:, columns(h)], scalar=float(2 * CAP // NBL + i), in1=tokh[:, columns(h)],
                                                   op0=ALU.is_equal, op1=ALU.mult).then_inc(q["w_tok"], 1)

            def list_parts(h):
                e0, e1 = PARTS[h]
                dve.wait_ge(q["t_list"], h + 1)
                nc.vector.tensor_copy(tokp[:, e0:e1], psJ[:, NA * e0:NA * e1].rearrange("p (e a) -> p e a", a=NA)).then_inc(q["r_tok"], 1)

            def list_out(h):
                e0, e1 = PARTS[h]
                dve.wait_ge(q["t_idx"], h + 1)
                nc.vector.tensor_scalar(idx[:, e0:e1], psT[:, 1, 0:(e1 - e0) * NI].rearrange("p (e i) -> p e i", i=NI),
                                        float(T // 2), None, ALU.add).then_inc(q["l_ld"], 1)

            one_hot_low(0)
            one_hot_high(0, 0, NA)
            one_hot_low(1, 0, 10)
            list_parts(0)
            one_hot_low(1, 10, 12)
            list_out(0)
            one_hot_low(1, 12, NBL)
            one_hot_high(1, 0, NA)
            list_parts(1)
            list_out(1)
            for e in range(E):
                dve.wait_ge(q["t_yo"], NB + e + 1)
                dve.wait_ge(g_ld[e % NG], 16 * NI * (e // NG + 1))
                if e < 2:
                    dve.wait_ge(o_st[e % 2], 16 * (NB // 2))
                else:
                    dve.wait_ge(sc_st[e % 2], 16 * NI * (e // 2))
                nc.vector.tensor_tensor(yo[:, e % 2], psT[:, 0].rearrange("p (a d) -> p a d", a=NI),
                                        gx[:, e % NG, :, D + e:D + e + 1].to_broadcast([P, NI, D]), ALU.mult).then_inc(q["v_yo"], 1)

        @block.tensor
        def _(pe):
            mm, tr = nc.tensor.matmul, nc.tensor.transpose
            pe.wait_ge(q["c_ld"], 16)
            pe.wait_ge(q["br_ld"], 16)
            tr(psJ[:, 0:NR], bias_rows[:], ident[0:NR, 0:NR]).then_inc(q["pe_bias"], 1)
            pe.wait_ge(q["bias_ok"], 1)
            pe.wait_ge(q["w_ld"], 16)
            mm(psJ[:, 0:1], wo, bias_c[:, R_BV:R_BV + 1], start=True, stop=True).then_inc(q["bo2_mm"], 1)
            pe.wait_ge(q["bo2_ok"], 1)

            def logits_even(s, pr):
                wait(pe, "v_sub", 2 * s.u(-1) + pr + 1)
                for bank in range(2):
                    m = maskr[:, bass.ds(UT * s.u(0) + pr, 1), :].to_broadcast([2, 8, S])
                    mm(psS[:, 2 * pr + bank], ind[:], m, start=True, stop=False, skip_group_check=True)
                logits_of(s, pr, (0, 2), False).then_inc(q["t_S0"], 1)

            def logits_odd(s, pr):
                wait(pe, "t_S0", 2 * s.u(0) + pr + 1)
                logits_of(s, pr, (1, 3), True).then_inc(q["t_S"], 1)

            def logits_of(s, pr, groups, stop):
                p = s.par(0)
                for g in groups:
                    for b in range(2):
                        r, c = 32 * g, P * pr + 64 * b
                        ins = mm(psS[64 * b:64 * b + 64, 2 * pr + g // 2, 256 * (g % 2):256 * (g % 2) + 256],
                                 QT[r:r + 32, p, c:c + 64], Kbd[r:r + 32, p, :, c:c + 64], start=False, stop=stop,
                                 tile_position=(r, 64 * b), skip_group_check=True)
                return ins

            def p_transpose(s, pr, hf):
                v = 4 * s.u(-1) + 2 * pr + hf
                wait(pe, "pl_pn", 2 * s.u(-1) + pr + 1)
                wait(pe, "a_pt", v - 1)
                for a in range(4):
                    k = 4 * hf + a
                    ins = tr(psT[:, hf, P * a:P * a + P], Pn[:, s.par(-1), pr, P * k:P * k + P], ident)
                ins.then_inc(q["t_T"], 1)

            def p_v(s, pr):
                wait(pe, "a_pt", 4 * s.u(-1) + 2 * pr + 2)
                wait(pe, "a_v", s.u(0))
                wait(pe, "v_v", s.u(0))
                wait(pe, "a_o", s.u(-1))
                for b in range(2):
                    for t in range(4):
                        o = P * (2 * pr + b)
                        ins = mm(psO[32 * t:32 * t + 32, o:o + P], Vz[:, s.par(-1), 2 * pr + b, 32 * t:32 * t + 32],
                                 PTs[:, pr, 2 * t:2 * t + 2, 64 * b:64 * b + 64], start=True, stop=True,
                                 tile_position=(0, 32 * t), skip_group_check=True)
                ins.then_inc(q["t_O"], 1)

            def hidden(n, m):
                e = n - NB
                if n < NB and m == 0:
                    pe.wait_ge(q["pl_x2"], FB // (UT * P) * (n + 1))
                if n == 0:
                    pe.wait_ge(q["v_sub"], 2 * NU)
                    pe.wait_ge(q["wf_ld"], 32)
                else:
                    pe.wait_ge(q["a_h"], NM * (n - 1) + m + 1)
                if e >= 0 and m == 0:
                    pe.wait_ge(q["a_xe"], e + 1)
                    pe.wait_ge(q["we_ld"], 16 * (1 + E))
                w = ws1[:, P * m:P * m + P] if e < 0 else w1[:, e, P * m:P * m + P]
                src = X2T[:, FB * n:FB * n + FB] if e < 0 else xeT[:, e % 2]
                mm(psS[:, m], w, src, start=True, stop=True).then_inc(q["t_h"], 1)

            def second(n, m):
                pe.wait_ge(q["a_h"], NM * n + m + 1)
                if m == 0:
                    wait(pe, "a_yy", n)
                    if n == 0:
                        pe.wait_ge(q["a_o"], NU)
                w = ws2[:, m] if n < NB else w2[:, n - NB, m]
                mm(psO[:], w, hT[:, m], start=(m == 0), stop=(m == NM - 1)).then_inc(q["t_yy"], 1)

            def turn_back(n):
                pe.wait_ge(q["a_yy"], n + 1)
                if n == 0:
                    pe.wait_ge(q["v_gate"], NU)
                wait(pe, "a_ys", min(n, NB))
                wait(pe, "v_yo", n - NB)
                for i in range(NI):
                    ins = tr(psT[:, 0, P * i:P * i + P], yT[:, P * i:P * i + P], ident)
                ins.then_inc(q["t_yo"], 1)

            def by_tile():
                pe.wait_ge(q["r_p"], 1)
                for h in range(2):
                    ins = tr(psT[:, 1, P * h:P * h + P], pr8[:, 16 * h:16 * h + 16, :].rearrange("p c e -> p (c e)"), ident)
                ins.then_inc(q["r_tT"], 1)

            def search(k):
                if k == 0:
                    pe.wait_ge(q["r_prT"], 1)
                pe.wait_ge(q["s_cnt"], 3 * (k + 1))
                pe.wait_ge(q["s_upd"], 2 + 3 * (k - 1) + 1 if k else 2)
                mm(psT[:, 1, 0:4], same[:], cnt[:], start=True, stop=True).then_inc(q["s_tot"], 1)

            def quarter(n, m):
                hidden(n, m)
                if n and n != NB:
                    if m < 2:
                        second(n - 1, 2 + m)
                    elif m == 2:
                        turn_back(n - 1)
                if m >= 2:
                    second(n, m - 2)

            def body(s):
                if not s.looped and s.u0 == 0:
                    pe.wait_ge(q["cdve"], 7)
                    pe.wait_ge(q["mrow"], 1)
                if s.on(0):
                    wait(pe, "a_q", s.u(1))
                    wait(pe, "pl_kbd", s.u(1))
                    logits_even(s, 0)
                    wait(pe, "a_v", s.u(1))
                    wait(pe, "v_v", s.u(1))
                if s.on(-2):
                    if not s.on(0):
                        wait(pe, "a_x2t", s.u(-3))
                    wait(pe, "a_o", s.u(-1))
                    for k in range(2):
                        ins = mm(psJ[:, 0:UT * P], wom[:, k], OLn[:, s.par(-2), :, 64 * k:64 * k + 64], start=(k == 0), stop=(k == 1))
                    ins.then_inc(q["t_y"], 1)
                    fill(s, "y", quarter)
                if s.on(0):
                    logits_odd(s, 0)
                if s.on(-2):
                    wait(pe, "a_y", s.u(-1))
                    for t in range(UT):
                        ins = tr(psJ[:, P * t:P * t + P], yTs[:, s.par(-2), P * t:P * t + P], ident)
                    ins.then_inc(q["t_yt"], 1)
                    fill(s, "yt", quarter)
                if s.on(0):
                    logits_even(s, 1)
                if s.on(1):
                    wait(pe, "v_x1", s.u(-1))
                    wait(pe, "v_xh1", s.u(2))
                    wait(pe, ctx_ld[s.par(1)], 16 * (s.half(1) + 1))
                    for t in range(UT):
                        tr(psJ[:, P * t:P * t + P], xh1[:, s.par(1), t], ident)
                    for t in range(UT):
                        ins = tr(psJ[:, P * (UT + t):P * (UT + t) + P], cin[:, s.par(1), t], ident)
                    ins.then_inc(q["t_xt"], 1)
                if s.on(0):
                    logits_odd(s, 1)
                if s.on(-1):
                    wait(pe, "v_gate", s.u(-3))
                    p_transpose(s, 0, 0)
                    p_transpose(s, 0, 1)
                if s.on(1):
                    wait(pe, "a_xt", s.u(2))
                    for k in range(2):
                        ins = mm(psJ[:, UT * P * k:UT * P * (k + 1)], wqkv[:, k], xcT[:, s.par(1), UT * k:UT * k + UT], start=True, stop=True)
                    ins.then_inc(q["t_qk"], 1)
                if s.on(-1):
                    p_transpose(s, 1, 0)
                    p_transpose(s, 1, 1)
                if s.on(1):
                    wait(pe, "a_q", s.u(2))
                    wait(pe, "a_k", s.u(2))
                elif s.on(-2):
                    wait(pe, "v_x1", s.u(-1))
                if s.on(-3):
                    wait(pe, "v_xh2", s.u(-2))
                    for t in range(UT):
                        ins = tr(psJ[:, P * t:P * t + P], xh2[:, s.par(-3), t], ident)
                    ins.then_inc(q["t_x2t"], 1)
                    fill(s, "x2t", quarter)
                if s.on(-1):
                    p_v(s, 0)
                if s.on(1):
                    wait(pe, "a_x2t", s.u(-2))
                    for b in range(4):
                        cT = xcT[:, s.par(1), UT + b // 2, 64 * (b % 2):64 * (b % 2) + 64]
                        for h in range(2):
                            ins = mm(psJ[64 * h:64 * h + 64, P * b:P * b + P], cT, wqkv[:, 2], start=True, stop=True,
                                     tile_position=(0, 64 * h), skip_group_check=True)
                    ins.then_inc(q["t_v"], 1)
                if s.on(-1):
                    p_v(s, 1)
                if s.on(-3):
                    wait(pe, "a_x2t", s.u(-2))
                    wait(pe, "a_pt", 4 * s.u(0) - 1 if s.on(-1) else 4 * NU)
                    if not s.on(-1):
                        wait(pe, "v_gate", s.u(-3))
                    for t in range(UT):
                        ins = mm(psT[:, 0, E * t:E * t + E], x2Ts[:, s.par(-3), P * t:P * t + P], gate_w, start=True, stop=True)
                    ins.then_inc(q["t_g"], 1)
                    fill(s, "g", quarter)

            pipeline(pe, body)

            def gather_in(e):
                pe.wait_ge(g_ld[e % NG], 16 * NI * (e // NG + 1))
                wait(pe, "a_xe", e)
                for i in range(NI):
                    ins = tr(psT[:, 1, P * i:P * i + P], gx[:, e % NG, i, 0:D], ident)
                ins.then_inc(q["t_xe"], 1)

            fl = lambda a: a[:].rearrange("p e c -> p (e c)")

            def thresholds():
                pe.wait_ge(q["s_fin"], 1)
                tr(psT[:, 1, 0:P], thr_b[:], ident).then_inc(q["t_thr"], 1)

            def ranks_equal():
                pe.wait_ge(q["r_m"], 2)
                pe.wait_ge(q["a_x2t"], NU)
                mm(psJ[:, 0:E * NT], tri[:], fl(eqm), start=True, stop=True)
                mm(psJ[:, E * NT:2 * E * NT], ones[:], fl(eqm), start=True, stop=True)
                mm(psT[:, 1, 0:E * NT], ones[:], fl(gtm), start=True, stop=True).then_inc(q["r_ranks"], 1)

            def ranks_chosen():
                pe.wait_ge(q["r_m"], 3)
                mm(psJ[:, 0:E * NT], tri[:], fl(selm), start=True, stop=True)
                mm(psJ[:, E * NT:2 * E * NT], ones[:], fl(selm), start=True, stop=True).then_inc(q["r_ranks"], 1)

            def token_lists(h):
                pe.wait_ge(q["b_oh"], NBL * (h + 1))
                pe.wait_ge(q["w_tok"], NA * (h + 1))
                pe.wait_ge(q["r_ranks2"], 2)
                for e in range(*PARTS[h]):
                    for c in range(NT):
                        g = c % 4
                        ins = mm(psJ[NBL * g:NBL * (g + 1), NA * e:NA * (e + 1)], Boh[:, :, NT * e + c], Awt[:, :, NT * e + c],
                                 start=(c < 4), stop=(c >= NT - 4), tile_position=(0, NBL * g), skip_group_check=True)
                ins.then_inc(q["t_list"], 1)

            def spread_lists(h):
                pe.wait_ge(q["r_tok"], h + 1)
                wait(pe, "l_ld", h)
                e0, e1 = PARTS[h]
                for j in range(NI):
                    ins = mm(psT[NBL * j:NBL * (j + 1), 1, 0:(e1 - e0) * NI], cst[:, C_STK:C_STK + NBL],
                             tokp[:, e0:e1, NI * j:NI * (j + 1)],
                             start=True, stop=True, tile_position=(0, NBL * j), skip_group_check=True)
                ins.then_inc(q["t_idx"], 1)

            for k in range(NM * NB - 6):
                if k == 0:
                    by_tile()
                elif k <= SEARCH:
                    search(k - 1)
                elif k == SEARCH + 1:
                    thresholds()
                elif k == SEARCH + 2:
                    ranks_equal()
                elif k == SEARCH + 4:
                    ranks_chosen()
                elif k == SEARCH + 8:
                    token_lists(0)
                    spread_lists(0)
                quarter((k + 6) // NM, (k + 6) % NM)
            second(NB - 1, 2)
            second(NB - 1, 3)
            pe.wait_ge(q["l_ld"], 1)

            gather_in(0)
            turn_back(NB - 1)
            for e in range(E):
                for m in range(NM):
                    quarter(NB + e, m)
                    if e == 0:
                        if m == 0:
                            token_lists(1)
                        elif m == 1:
                            spread_lists(1)
                        elif m == 2:
                            pe.wait_ge(q["l_ld"], 2)
                            gather_in(1)
                    elif m == 2 and e + 1 < E:
                        gather_in(e + 1)
            second(NB + E - 1, 2)
            second(NB + E - 1, 3)
            turn_back(NB + E - 1)


def kernel(**inputs):
    import concourse.bacc as _bacc
    from concourse.bass_utils import run_bass_kernel_spmd as _run

    a = {n: np.ascontiguousarray(v) for n, v in inputs.items()}
    small = [a["L0_xattn_" + n] for n in ("Wq", "Wk", "Wv", "Wo")] + [a["L0_ffn_gate"]]
    rows = [a["L0_ffn_" + n] for n in ("b1", "bs1", "b2", "bs2")] + [a["L0_xattn_" + n] for n in ("bq", "bk", "bv", "bo")]
    consts, kbits = constants()
    arrays = {"x": a["x"], "ctx": a["ctx_1024"], "mask": a["mask_BxS2_bf1"].view(np.uint8),
              "W1": a["L0_ffn_W1"], "W2": a["L0_ffn_W2"], "Ws1": a["L0_ffn_Ws1"], "Ws2": a["L0_ffn_Ws2"],
              "weights": np.concatenate(small, axis=1), "biases": np.concatenate([r.reshape(-1, P) for r in rows]),
              "consts": consts, "kbits": kbits}
    nc = _bacc.Bacc("TRN2", target_bir_lowering=False, num_devices=1)
    args = [nc.dram_tensor(n, v.shape, mybir.dt.from_np(v.dtype), kind="ExternalInput").ap() for n, v in arrays.items()]
    args.append(nc.dram_tensor("out", (B, S, D), F32, kind="ExternalOutput").ap())
    args.append(nc.dram_tensor("gather_table", (T, ROW), F32).ap())
    build(nc, *args)
    r = _run(nc, [arrays], core_ids=[0])
    return r.results[0]["out"]
```
